# Optimizing a Trainium2 kernel written in Bass

```python
import numpy as np
import jax
import jax.numpy as jnp

def _softmax(x, axis=-1):
    return jax.nn.softmax(x, axis=axis)

def _gelu(x):
    return jax.nn.gelu(x, approximate=True)

def _silu(x):
    return jax.nn.silu(x)

def _sigmoid(x):
    return jax.nn.sigmoid(x)

def _layernorm(x, axis=-1, eps=1e-05):
    m = jnp.mean(x, axis=axis, keepdims=True)
    v = jnp.var(x, axis=axis, keepdims=True)
    return (x - m) / jnp.sqrt(v + eps)

def _scatter_add(tgt, idx, src, axis=0):
    return tgt.at[idx].add(src)

def _segment_sum(src, seg, n):
    return jax.ops.segment_sum(src, seg, n)
kernel_name = 'mk_seq_preln_d1_jaxref_r8_008e20'

def setup_inputs(seed: int=0):
    np.random.seed(seed)
    _w = jnp.asarray

    def _L0_attn_setup():
        import jax, jax.numpy as jnp
        from jax import lax
        import numpy as np
        DIM = 128
        HIDDEN = 256
        DSTATE = 16
        DRANK = 64
        K = 4
        N, T = (2, 128)

        def _s6_forward(x, W_in, conv_w, conv_b, W_gate, W_delta, delta_bias, A_log, D, W_out):
            uo = x @ W_in.T
            u, o = (uo[..., :HIDDEN], uo[..., HIDDEN:])
            uc = lax.conv_general_dilated(u.transpose(0, 2, 1), conv_w, (1,), [(K - 1, 0)], feature_group_count=HIDDEN, dimension_numbers=('NCH', 'OIH', 'NCH'))
            u = jax.nn.silu((uc + conv_b[None, :, None]).transpose(0, 2, 1))
            g = u @ W_gate.T
            delta_lo = g[..., :DRANK]
            b = g[..., DRANK:DRANK + DSTATE]
            c = g[..., DRANK + DSTATE:]
            delta = jax.nn.softplus(delta_lo @ W_delta.T + delta_bias)
            A = -jnp.exp(A_log)

            def step(h, inp):
                d_t, u_t, b_t, c_t = inp
                forget = jnp.exp(A * d_t[..., None])
                h = forget * h + (d_t * u_t)[..., None] * b_t[:, None, :]
                y_t = jnp.einsum('nhs,ns->nh', h, c_t)
                return (h, y_t)
            h0 = jnp.zeros((x.shape[0], HIDDEN, DSTATE), x.dtype)
            xs = (delta.transpose(1, 0, 2), u.transpose(1, 0, 2), b.transpose(1, 0, 2), c.transpose(1, 0, 2))
            _, ys = lax.scan(step, h0, xs)
            y = ys.transpose(1, 0, 2) + D * u
            y = y * jax.nn.sigmoid(o) * o
            return y @ W_out.T
        key = jax.random.key(seed)
        ks = jax.random.split(key, 8)
        x = jax.random.normal(ks[0], (N, T, DIM), jnp.float32)
        s_in = DIM ** (-0.5)
        W_in = jax.random.uniform(ks[1], (2 * HIDDEN, DIM), jnp.float32, -s_in, s_in)
        s_h = HIDDEN ** (-0.5)
        W_gate = jax.random.uniform(ks[2], (DRANK + 2 * DSTATE, HIDDEN), jnp.float32, -s_h, s_h)
        s_d = DRANK ** (-0.5)
        W_delta = jax.random.uniform(ks[3], (HIDDEN, DRANK), jnp.float32, -s_d, s_d)
        W_out = jax.random.uniform(ks[4], (DIM, HIDDEN), jnp.float32, -s_h, s_h)
        s_k = K ** (-0.5)
        conv_w = jax.random.uniform(ks[5], (HIDDEN, 1, K), jnp.float32, -s_k, s_k)
        conv_b = jax.random.uniform(ks[6], (HIDDEN,), jnp.float32, -s_k, s_k)
        dt_max, dt_min = (np.log(0.1), np.log(0.001))
        dt = jnp.exp(jax.random.uniform(ks[7], (HIDDEN,), jnp.float32) * (dt_max - dt_min) + dt_min)
        dt = jnp.clip(dt, 0.0001)
        delta_bias = dt + jnp.log(-jnp.expm1(-dt))
        A_log = jnp.broadcast_to(jnp.log(jnp.arange(1, DSTATE + 1, dtype=jnp.float32)), (HIDDEN, DSTATE)).copy()
        D = jnp.ones((HIDDEN,), jnp.float32)
        return dict(x=x, W_in=W_in, conv_w=conv_w, conv_b=conv_b, W_gate=W_gate, W_delta=W_delta, delta_bias=delta_bias, A_log=A_log, D=D, W_out=W_out)
    _L0_attn_in = _L0_attn_setup()

    def _L0_ffn_setup():
        import jax, jax.numpy as jnp
        import numpy as np
        B, S, D = (1, 256, 128)
        E, K, F = (8, 2, 176)
        NS = 2
        SCALE = 2.5

        def _swiglu_mlp(x, wg, wu, wd):
            return jax.nn.silu(x @ wg) * (x @ wu) @ wd
        key = jax.random.key(seed)
        ks = jax.random.split(key, 8)
        s = 0.02
        return {'hidden_states': jax.random.normal(ks[0], (B, S, D), jnp.float32), 'gate_w': jax.random.normal(ks[1], (E, D), jnp.float32) * s, 'w_gate': jax.random.normal(ks[2], (E, D, F), jnp.float32) * s, 'w_up': jax.random.normal(ks[3], (E, D, F), jnp.float32) * s, 'w_down': jax.random.normal(ks[4], (E, F, D), jnp.float32) * s, 'sw_gate': jax.random.normal(ks[5], (D, F * NS), jnp.float32) * s, 'sw_up': jax.random.normal(ks[6], (D, F * NS), jnp.float32) * s, 'sw_down': jax.random.normal(ks[7], (F * NS, D), jnp.float32) * s}
    _L0_ffn_in = _L0_ffn_setup()
    _d = {'L0_attn_x': _L0_attn_in['x'], 'L0_attn_W_in': _L0_attn_in['W_in'], 'L0_attn_conv_w': _L0_attn_in['conv_w'], 'L0_attn_conv_b': _L0_attn_in['conv_b'], 'L0_attn_W_gate': _L0_attn_in['W_gate'], 'L0_attn_W_delta': _L0_attn_in['W_delta'], 'L0_attn_delta_bias': _L0_attn_in['delta_bias'], 'L0_attn_A_log': _L0_attn_in['A_log'], 'L0_attn_D': _L0_attn_in['D'], 'L0_attn_W_out': _L0_attn_in['W_out'], 'L0_ffn_gate_w': _L0_ffn_in['gate_w'], 'L0_ffn_w_gate': _L0_ffn_in['w_gate'], 'L0_ffn_w_up': _L0_ffn_in['w_up'], 'L0_ffn_w_down': _L0_ffn_in['w_down'], 'L0_ffn_sw_gate': _L0_ffn_in['sw_gate'], 'L0_ffn_sw_up': _L0_ffn_in['sw_up'], 'L0_ffn_sw_down': _L0_ffn_in['sw_down']}
    _x0 = _d['L0_attn_x']
    _d['L0_attn_x'] = jax.random.normal(jax.random.fold_in(jax.random.key(seed), 1), (32, 256, 128), dtype=_x0.dtype)
    del _x0
    return _d

def reference(L0_attn_x, L0_attn_W_in, L0_attn_conv_w, L0_attn_conv_b, L0_attn_W_gate, L0_attn_W_delta, L0_attn_delta_bias, L0_attn_A_log, L0_attn_D, L0_attn_W_out, L0_ffn_gate_w, L0_ffn_w_gate, L0_ffn_w_up, L0_ffn_w_down, L0_ffn_sw_gate, L0_ffn_sw_up, L0_ffn_sw_down):

    def _L0_attn_ref(x, W_in, conv_w, conv_b, W_gate, W_delta, delta_bias, A_log, D, W_out):
        import jax, jax.numpy as jnp
        from jax import lax
        import numpy as np
        DIM = 128
        HIDDEN = 256
        DSTATE = 16
        DRANK = 64
        K = 4
        N, T = (2, 128)

        def _s6_forward(x, W_in, conv_w, conv_b, W_gate, W_delta, delta_bias, A_log, D, W_out):
            uo = x @ W_in.T
            u, o = (uo[..., :HIDDEN], uo[..., HIDDEN:])
            uc = lax.conv_general_dilated(u.transpose(0, 2, 1), conv_w, (1,), [(K - 1, 0)], feature_group_count=HIDDEN, dimension_numbers=('NCH', 'OIH', 'NCH'))
            u = jax.nn.silu((uc + conv_b[None, :, None]).transpose(0, 2, 1))
            g = u @ W_gate.T
            delta_lo = g[..., :DRANK]
            b = g[..., DRANK:DRANK + DSTATE]
            c = g[..., DRANK + DSTATE:]
            delta = jax.nn.softplus(delta_lo @ W_delta.T + delta_bias)
            A = -jnp.exp(A_log)

            def step(h, inp):
                d_t, u_t, b_t, c_t = inp
                forget = jnp.exp(A * d_t[..., None])
                h = forget * h + (d_t * u_t)[..., None] * b_t[:, None, :]
                y_t = jnp.einsum('nhs,ns->nh', h, c_t)
                return (h, y_t)
            h0 = jnp.zeros((x.shape[0], HIDDEN, DSTATE), x.dtype)
            xs = (delta.transpose(1, 0, 2), u.transpose(1, 0, 2), b.transpose(1, 0, 2), c.transpose(1, 0, 2))
            _, ys = lax.scan(step, h0, xs)
            y = ys.transpose(1, 0, 2) + D * u
            y = y * jax.nn.sigmoid(o) * o
            return y @ W_out.T
        return _s6_forward(x, W_in, conv_w, conv_b, W_gate, W_delta, delta_bias, A_log, D, W_out)

    def _L0_ffn_ref(hidden_states, gate_w, w_gate, w_up, w_down, sw_gate, sw_up, sw_down):
        import jax, jax.numpy as jnp
        import numpy as np
        B, S, D = (1, 256, 128)
        E, K, F = (8, 2, 176)
        NS = 2
        SCALE = 2.5

        def _swiglu_mlp(x, wg, wu, wd):
            return jax.nn.silu(x @ wg) * (x @ wu) @ wd
        identity = hidden_states
        x = hidden_states.reshape(-1, hidden_states.shape[-1])
        T = x.shape[0]
        logits = x.astype(jnp.float32) @ gate_w.astype(jnp.float32).T
        scores = jax.nn.softmax(logits, axis=-1)
        topk_w, topk_i = jax.lax.top_k(scores, K)
        topk_w = topk_w / (topk_w.sum(-1, keepdims=True) + 1e-20) * SCALE
        combine = jnp.zeros((T, E), jnp.float32).at[jnp.arange(T)[:, None], topk_i].set(topk_w)
        g = jax.nn.silu(jnp.einsum('td,edf->etf', x, w_gate)) * jnp.einsum('td,edf->etf', x, w_up)
        expert_out = jnp.einsum('etf,efd->etd', g, w_down)
        y = jnp.einsum('te,etd->td', combine, expert_out).astype(x.dtype)
        y = y.reshape(identity.shape)
        return y + _swiglu_mlp(identity, sw_gate, sw_up, sw_down)
    x = L0_attn_x
    x = x + _L0_attn_ref(_layernorm(x, axis=-1), L0_attn_W_in, L0_attn_conv_w, L0_attn_conv_b, L0_attn_W_gate, L0_attn_W_delta, L0_attn_delta_bias, L0_attn_A_log, L0_attn_D, L0_attn_W_out)
    x = x + _L0_ffn_ref(_layernorm(x, axis=-1), L0_ffn_gate_w, L0_ffn_w_gate, L0_ffn_w_up, L0_ffn_w_down, L0_ffn_sw_gate, L0_ffn_sw_up, L0_ffn_sw_down)
    return x

_drawn_inputs = setup_inputs


def setup_inputs(seed=0):
    import zlib

    import numpy as np

    out = dict(_drawn_inputs(seed))
    spreads = {'L0_attn_D': (1.0, 0.6)}
    factors = {'L0_attn_W_gate': 8.0,
     'L0_attn_W_delta': 8.0,
     'L0_attn_delta_bias': 8.0,
     'L0_attn_A_log': 8.0,
     'L0_ffn_gate_w': 5.296,
     'L0_ffn_w_gate': 4.663,
     'L0_ffn_w_up': 4.622,
     'L0_ffn_w_down': 4.622,
     'L0_ffn_sw_gate': 5.855,
     'L0_ffn_sw_up': 5.833,
     'L0_ffn_sw_down': 5.844}
    for name, (base, spread) in spreads.items():
        noise = np.random.default_rng([zlib.crc32(name.encode()), seed]).standard_normal(out[name].shape)
        drawn = base * np.exp(spread * noise) if base else spread * noise
        out[name] = jnp.asarray(drawn.astype(out[name].dtype))
    for name, factor in factors.items():
        out[name] = (out[name] * factor).astype(out[name].dtype)
    return out
```

```python
from contextlib import ExitStack

import concourse.bass as bass
from concourse import mybir

ALU = mybir.AluOpType
ACT = mybir.ActivationFunctionType
AX = mybir.AxisListType
F32 = mybir.dt.float32
BF16 = mybir.dt.bfloat16

P = 128
SEQS, T, DIM = 32, 256, 128
HIDDEN, STATES, RANK, TAPS = 256, 16, 64, 4
HALVES = HIDDEN // P
TILES = T // P
CH = P // STATES
JB = P // 32
GROUPS = 8
IN_HALF = GROUPS // HALVES
EXPERTS, WIDTH, SHARED = 8, 176, 352
ROUTED = EXPERTS * WIDTH
FEATURES = ROUTED + SHARED
RCHUNKS = ROUTED // P
CHUNKS = -(-FEATURES // P)
LAST = FEATURES - (CHUNKS - 1) * P
ORDER = list(range(RCHUNKS, CHUNKS)) + list(range(RCHUNKS))
PAIRS = (RCHUNKS + 1) // 2
PARTS = 3
EPS = 1e-5
SCALE = 2.5
WEIGHT_STEPS = 7 * HALVES + 6
GU_SLOT = [0, 0, 0, 2, 4, 4, 4, 0]
DN_SLOT = [0, 0, 0, 0, 0, 3, 0, 11]
PAIR_SLOT = [0, 0, 0, 0, 0, 2, 4, 0]


def spread(counts, slot):
    first = sum(counts[:slot])
    return range(first, first + counts[slot])


def rows(chunk):
    return P if chunk < CHUNKS - 1 else LAST


def build(nc, x, W_in, conv_w, conv_b, W_gate, W_delta, delta_bias, A_log, Dskip, W_out,
          gate_w, w_gate, w_up, w_down, sw_gate, sw_up, sw_down, out):
    with ExitStack() as ctx:
        def sb(name, shape, dt=F32):
            return ctx.enter_context(nc.sbuf_tensor(name, shape, dt))

        def sem(name):
            return ctx.enter_context(nc.semaphore(name))

        win_rows = sb("win_rows", [P, 2 * HALVES, DIM])
        taps = sb("taps", [P, HALVES, TAPS])
        wconv_rows = sb("wconv_rows", [P, HALVES, TAPS, DIM])
        wgate_rows = sb("wgate_rows", [RANK + 2 * STATES, HIDDEN])
        wdelta_rows = sb("wdelta_rows", [P, HALVES, RANK])
        wout_rows = sb("wout_rows", [DIM, HIDDEN])
        router_rows = sb("router_rows", [EXPERTS, DIM])
        conv_bias = sb("conv_bias", [P, HALVES])
        conv_bias_half = sb("conv_bias_half", [P, HALVES])
        delta_b = sb("delta_b", [P, HALVES])
        skip_half = sb("skip_half", [P, HALVES])
        vector_rows = sb("vector_rows", [3 * HALVES, P])
        a_log_rows = sb("a_log_rows", [HIDDEN // CH, P])
        neg_a = sb("neg_a", [P, HIDDEN // CH])
        wconv = sb("wconv", [DIM, HALVES, TAPS, P])
        wo = sb("wo", [DIM, HALVES, P])
        wlow = sb("wlow", [P, HALVES, RANK])
        wbc = sb("wbc", [P, 2, HALVES, CH, STATES])
        wdelta = sb("wdelta", [RANK, HALVES, P])
        wout = sb("wout", [P, HALVES, DIM])
        router = sb("router", [DIM, EXPERTS])
        ffn_gate = sb("ffn_gate", [DIM, FEATURES])
        ffn_up = sb("ffn_up", [DIM, FEATURES])
        ffn_down = sb("ffn_down", [P, CHUNKS, DIM])
        ident = sb("ident", [P, P])
        ident_bf = sb("ident_bf", [P, P], BF16)
        spread_sel = sb("spread_sel", [PARTS * 32, IN_HALF, CH, STATES], BF16)
        sum_sel = sb("sum_sel", [P, IN_HALF, 32])
        expert_sel = sb("expert_sel", [PARTS * EXPERTS, ROUTED], BF16)
        before = sb("before", [P, EXPERTS, EXPERTS])
        exponent = sb("exponent", [P, TILES])
        x_in = [sb(f"x_in{i}", [P, TILES, DIM]) for i in range(2)]
        stats1 = sb("stats1", [P, TILES, 6])
        mean_var1 = sb("mean_var1", [P, TILES, 2])
        var1 = sb("var1", [P, TILES])
        rstd1 = sb("rstd1", [P, TILES])
        xn = sb("xn", [P, TILES, DIM])
        xnT = sb("xnT", [DIM, TAPS - 1 + T])
        conv_out = sb("conv_out", [P, HALVES, T])
        conv_tanh = sb("conv_tanh", [P, HALVES, T])
        u2 = [sb(f"u2_{i}", [P, HALVES, T]) for i in range(2)]
        gate_tanh = sb("gate_tanh", [P, HALVES, T])
        gate2 = [sb(f"gate2_{i}", [P, HALVES, T]) for i in range(2)]
        bc = [sb(f"bc_{i}", [P, 2, T]) for i in range(2)]
        low = sb("low", [RANK, T])
        z_abs = sb("z_abs", [P, HALVES, T])
        z_exp = sb("z_exp", [P, HALVES, T])
        z_log = sb("z_log", [P, HALVES, T])
        z_relu = sb("z_relu", [P, HALVES, T])
        lost = sb("lost", [P, HALVES, T])
        kept = sb("kept", [P, HALVES, T])
        delta_du = sb("delta_du", [P, HALVES, 2 * T])
        rest = sb("rest", [P, HALVES, 2 * T])
        parts = [sb(f"part{i}", [P, HALVES, 2 * T], BF16) for i in range(PARTS)]
        packed = [sb(f"packed{i}", [PARTS * 32, HALVES, 2, JB, T], BF16) for i in range(2)]
        decay = [sb(f"decay{i}", [P, JB, T]) for i in range(2)]
        inject = [sb(f"inject{i}", [P, JB, T]) for i in range(2)]
        state = [sb(f"state{i}", [P, JB, T]) for i in range(2)]
        read = [sb(f"read{i}", [P, JB, T]) for i in range(2)]
        x_res = [sb(f"x_res{i}", [P, TILES, DIM]) for i in range(2)]
        y_skip = [sb(f"y_skip{i}", [P, HALVES, T]) for i in range(2)]
        y_gated = sb("y_gated", [P, HALVES, T])
        x1 = sb("x1", [P, TILES, DIM])
        stats2 = sb("stats2", [P, TILES, 6])
        mean_var2 = sb("mean_var2", [P, TILES, 2])
        var2 = sb("var2", [P, TILES])
        rstd2 = sb("rstd2", [P, TILES])
        xn2 = sb("xn2", [P, TILES, DIM])
        xn2T = sb("xn2T", [DIM, T])
        logit = sb("logit", [P, TILES, EXPERTS])
        above = sb("above", [P, TILES, EXPERTS, EXPERTS])
        above_eq = sb("above_eq", [P, TILES, EXPERTS, EXPERTS])
        tied = sb("tied", [P, TILES, EXPERTS, EXPERTS])
        ahead = sb("ahead", [P, TILES, EXPERTS, EXPERTS])
        rank = sb("rank", [P, TILES, EXPERTS])
        chosen = sb("chosen", [P, TILES, EXPERTS])
        top = sb("top", [P, TILES])
        shifted = sb("shifted", [P, TILES, EXPERTS])
        expd = sb("expd", [P, TILES, EXPERTS])
        total = sb("total", [P, TILES])
        picked = sb("picked", [P, TILES, EXPERTS])
        picked_sum = sb("picked_sum", [P, TILES])
        denom = sb("denom", [P, TILES])
        inv = sb("inv", [P, TILES])
        combine = sb("combine", [P, TILES, EXPERTS])
        comb_r1 = sb("comb_r1", [P, TILES, EXPERTS])
        comb_parts = sb("comb_parts", [P, TILES, PARTS * EXPERTS], BF16)
        combT = sb("combT", [PARTS * EXPERTS, T], BF16)
        comb_all = sb("comb_all", [P, 2 * PAIRS, T])
        g_tanh = [sb(f"g_tanh{i}", [P, T]) for i in range(2)]
        g_silu = [sb(f"g_silu{i}", [P, T]) for i in range(2)]
        h_raw = sb("h_raw", [P, CHUNKS, T])
        h = sb("h", [P, RCHUNKS, T])
        result = [sb(f"result{i}", [P, TILES, DIM]) for i in range(2)]

        spread_ps = ctx.enter_context(nc.psum_tensor("spread_ps", [P, 2, JB, T], F32))
        proj_ps = ctx.enter_context(nc.psum_tensor("proj_ps", [P, 512], F32))
        even_ps = ctx.enter_context(nc.psum_tensor("even_ps", [P, 512], F32))
        odd_ps = ctx.enter_context(nc.psum_tensor("odd_ps", [P, 512], F32))
        acc_ps = ctx.enter_context(nc.psum_tensor("acc_ps", [P, 512], F32))
        y_ps = acc_ps[:, 0:T]
        down_ps = acc_ps[:, T:2 * T]

        w_loaded = sem("w_loaded")
        ident_steps = sem("ident_steps")
        consts = sem("consts")
        copies_in = sem("copies_in")
        prep = sem("prep")
        prep_a = sem("prep_a")
        turned = sem("turned")
        weights_ready = sem("weights_ready")
        x_loaded = [sem(f"x_loaded{i}") for i in range(2)]
        ln1_stats = sem("ln1_stats")
        ln1_rstd = sem("ln1_rstd")
        ln1_done = sem("ln1_done")
        xnT_mm = sem("xnT_mm")
        xnT_done = sem("xnT_done")
        conv_mm = sem("conv_mm")
        conv_act = sem("conv_act")
        u_done = sem("u_done")
        gate_mm = sem("gate_mm")
        gate_act = sem("gate_act")
        gate_done = sem("gate_done")
        bc_mm = sem("bc_mm")
        bc_done = sem("bc_done")
        low_mm = sem("low_mm")
        low_done = sem("low_done")
        delta_mm = sem("delta_mm")
        z_abs_done = sem("z_abs_done")
        z_exp_done = sem("z_exp_done")
        z_log_done = sem("z_log_done")
        z_relu_done = sem("z_relu_done")
        kept_done = sem("kept_done")
        lost_done = sem("lost_done")
        delta_done = sem("delta_done")
        du_done = sem("du_done")
        hi_done = sem("hi_done")
        rest_done = sem("rest_done")
        mid_done = sem("mid_done")
        lo_done = sem("lo_done")
        packed_in = sem("packed_in")
        delta_spread = sem("delta_spread")
        du_spread = sem("du_spread")
        decay_done = sem("decay_done")
        inject_done = sem("inject_done")
        state_done = sem("state_done")
        read_done = sem("read_done")
        sum_done = sem("sum_done")
        y_taken = sem("y_taken")
        y_clear = sem("y_clear")
        res_loaded = [sem(f"res_loaded{i}") for i in range(2)]
        y_done = sem("y_done")
        proj_mm = sem("proj_mm")
        x1_done = sem("x1_done")
        ln2_stats = sem("ln2_stats")
        ln2_rstd = sem("ln2_rstd")
        ln2_done = sem("ln2_done")
        xn2T_mm = sem("xn2T_mm")
        xn2T_done = sem("xn2T_done")
        logit_mm = sem("logit_mm")
        rank_steps = sem("rank_steps")
        expd_done = sem("expd_done")
        comb_steps = sem("comb_steps")
        combT_mm = sem("combT_mm")
        combT_done = sem("combT_done")
        pair_mm = sem("pair_mm")
        pair_done = sem("pair_done")
        gu_mm = sem("gu_mm")
        tanh_done = sem("tanh_done")
        silu_done = sem("silu_done")
        h_done = sem("h_done")
        hc_done = sem("hc_done")
        down_mm = sem("down_mm")
        result_done = sem("result_done")
        down_clear = sem("down_clear")
        stored = [sem(f"stored{i}") for i in range(2)]

        x_t = x.rearrange("n (j p) d -> n p j d", p=P)
        out_t = out.rearrange("n (j p) d -> n p j d", p=P)

        setup_loads = [
            (win_rows[:], W_in.rearrange("(c p) d -> p c d", p=P)),
            (taps[:], conv_w.rearrange("(c p) o k -> p c (o k)", p=P)),
            (wgate_rows[:], W_gate),
            (wdelta_rows[:], W_delta.rearrange("(c p) r -> p c r", p=P)),
            (wout_rows[:], W_out),
            (router_rows[:], gate_w),
            (vector_rows[0:HALVES, :], conv_b.rearrange("(c p) -> c p", p=P)),
            (vector_rows[HALVES:2 * HALVES, :], delta_bias.rearrange("(c p) -> c p", p=P)),
            (vector_rows[2 * HALVES:, :], Dskip.rearrange("(c p) -> c p", p=P)),
            (a_log_rows[:], A_log.rearrange("(g c) s -> g (c s)", c=CH)),
            (ffn_gate[:, 0:ROUTED].rearrange("d (e f) -> d e f", e=EXPERTS), w_gate.rearrange("e d f -> d e f")),
            (ffn_gate[:, ROUTED:], sw_gate),
            (ffn_up[:, 0:ROUTED].rearrange("d (e f) -> d e f", e=EXPERTS), w_up.rearrange("e d f -> d e f")),
            (ffn_up[:, ROUTED:], sw_up),
            (ffn_down[:, 0:RCHUNKS, :], w_down.rearrange("e f d -> (e f) d").rearrange("(c p) d -> p c d", p=P)),
            (ffn_down[:, RCHUNKS:CHUNKS - 1, :],
             sw_down[0:SHARED - LAST, :].rearrange("(c p) d -> p c d", p=P)),
            (ffn_down[0:LAST, CHUNKS - 1, :], sw_down[SHARED - LAST:, :]),
        ]

        def steps(eng, body):
            body(-1, 0, True, False, False)
            body(0, 1, True, True, False)
            with eng.Fori(0, (SEQS - 2) // 2) as i:
                for odd in range(2):
                    body(2 * i + 1 + odd, odd, True, True, True)
            body(SEQS - 1, 0, False, True, True)
            body(SEQS, 1, False, False, True)

        def waiter(eng):
            def wait(semaphore, value):
                if not isinstance(value, int) or value > 0:
                    eng.wait_ge(semaphore, value)
            return wait

        turned_ps = spread_ps[:].rearrange("p w (g h) t -> p (w g) (h t)", h=2)
        turned_vectors = proj_ps[:, 16:16 + 3 * HALVES]
        turned_a = proj_ps[:, 32:32 + HIDDEN // CH]

        block = ctx.enter_context(nc.Block())

        @block.sync
        def _(sp):
            wait = waiter(sp)
            sp.dma_start(x_in[0][:], x_t[0]).then_inc(x_loaded[0], 16)
            for to, source in setup_loads:
                sp.dma_start(to, source).then_inc(w_loaded, 16)
            sp.wait_ge(consts, 7)
            for part in range(1, PARTS):
                sp.dma_start(expert_sel[part * EXPERTS:(part + 1) * EXPERTS, :],
                             expert_sel[0:EXPERTS, :]).then_inc(copies_in, 16)

            def body(k, b, project, scan, ffn):
                p, f = k + 1, k - 1
                if ffn:
                    wait(x1_done, f)
                    sp.dma_start(x_res[b][:], x_t[f]).then_inc(res_loaded[b], 16)
                if project:
                    wait(du_spread, GROUPS * k)
                    for part, ready in enumerate((hi_done, mid_done, lo_done)):
                        wait(ready, p + 1)
                        for j in range(JB):
                            sp.dma_start(packed[b][32 * part:32 * part + 32, :, :, j, :],
                                         parts[part][32 * j:32 * j + 32, :, :]
                                         .rearrange("p c (w t) -> p c w t", w=2)).then_inc(packed_in, 16)
                if ffn:
                    wait(result_done, f + 1)
                    sp.dma_start(out_t[f], result[b][:]).then_inc(stored[b], 16)

            def fetch(k, b):
                wait(ln1_done, k + 1)
                sp.dma_start(x_in[b][:], x_t[k + 2]).then_inc(x_loaded[b], 16)

            sp.dma_start(x_in[1][:], x_t[1]).then_inc(x_loaded[1], 16)
            body(-1, 0, True, False, False)
            fetch(0, 0)
            body(0, 1, True, True, False)
            with sp.Fori(0, (SEQS - 4) // 2) as i:
                for odd in range(2):
                    fetch(2 * i + 1 + odd, 1 - odd)
                    body(2 * i + 1 + odd, odd, True, True, True)
            k0 = SEQS - 3
            fetch(k0, 1)
            body(k0, 0, True, True, True)
            body(k0 + 1, 1, True, True, True)
            body(SEQS - 1, 0, False, True, True)
            body(SEQS, 1, False, False, True)
            for b in range(2):
                sp.wait_ge(stored[b], 16 * (SEQS // 2))

        @block.gpsimd
        def _(pool):
            wait = waiter(pool)
            pool.memset(ident[:], 0.0).then_inc(ident_steps, 1)
            pool.memset(sum_sel[:], 1.0).then_inc(ident_steps, 1)
            pool.memset(before[:], 0.0).then_inc(ident_steps, 1)
            pool.memset(exponent[:], -0.5).then_inc(ident_steps, 1)
            pool.wait_ge(ident_steps, 4)
            pool.affine_select(out=ident[:], in_=ident[:], compare_op=ALU.not_equal, fill=1.0, base=0,
                               pattern=[[-1, P]], channel_multiplier=1).then_inc(consts, 1)
            pool.affine_select(out=before[:], in_=before[:], compare_op=ALU.is_ge, fill=1.0, base=0,
                               pattern=[[-1, EXPERTS], [1, EXPERTS]], channel_multiplier=0).then_inc(consts, 1)
            pool.affine_select(out=sum_sel[:], in_=sum_sel[:], compare_op=ALU.is_ge, fill=0.0, base=0,
                               pattern=[[P, IN_HALF], [-STATES, 32]], channel_multiplier=1).then_inc(ident_steps, 1)
            pool.wait_ge(ident_steps, 5)
            pool.affine_select(out=sum_sel[:], in_=sum_sel[:], compare_op=ALU.is_ge, fill=0.0, base=STATES - 1,
                               pattern=[[-P, IN_HALF], [STATES, 32]], channel_multiplier=-1).then_inc(consts, 1)
            pool.wait_ge(consts, 3)
            pool.memset(spread_sel[:], 0.0).then_inc(ident_steps, 1)
            pool.wait_ge(ident_steps, 6)
            for part in range(PARTS):
                block_rows = spread_sel[32 * part:32 * part + 32, :, :, :]
                pool.affine_select(out=block_rows, in_=block_rows, compare_op=ALU.not_equal, fill=1.0, base=0,
                                   pattern=[[-CH, IN_HALF], [-1, CH], [0, STATES]],
                                   channel_multiplier=1).then_inc(consts, 1)
                pool.wait_ge(consts, 4 + part)
            pool.memset(expert_sel[0:EXPERTS, :], 1.0).then_inc(ident_steps, 1)
            pool.wait_ge(ident_steps, 7)
            pool.affine_select(out=expert_sel[0:EXPERTS, :], in_=expert_sel[0:EXPERTS, :], compare_op=ALU.is_ge,
                               fill=0.0, base=0, pattern=[[1, ROUTED]],
                               channel_multiplier=-WIDTH).then_inc(ident_steps, 1)
            pool.wait_ge(ident_steps, 8)
            pool.affine_select(out=expert_sel[0:EXPERTS, :], in_=expert_sel[0:EXPERTS, :], compare_op=ALU.is_ge,
                               fill=0.0, base=WIDTH - 1, pattern=[[-1, ROUTED]],
                               channel_multiplier=WIDTH).then_inc(consts, 1)
            pool.wait_ge(consts, 7)

            def body(k, b, project, scan, ffn):
                p, s, f = k + 1, k, k - 1
                other = 1 - b

                def rstd(var, rstd_t, var_sem, done, n):
                    wait(var_sem, 5 * n + 5)
                    pool.tensor_tensor(rstd_t[:], var[:], exponent[:], ALU.pow).then_inc(done, 1)

                for q in range(GROUPS):
                    if project and q == 0:
                        rstd(var1, rstd1, ln1_stats, ln1_rstd, p)
                    if ffn and q == 2:
                        rstd(var2, rstd2, ln2_stats, ln2_rstd, f)
                    if project and q == 4:
                        wait(kept_done, p + 1)
                        pool.tensor_tensor(lost[:], z_exp[:], kept[:], ALU.subtract).then_inc(lost_done, 1)
                        wait(lost_done, 2 * p + 1)
                        wait(z_relu_done, p + 1)
                        wait(delta_done, p)
                        pool.tensor_tensor(z_relu[:], z_relu[:], lost[:], ALU.add).then_inc(lost_done, 1)
                    if project and q == 5:
                        wait(hi_done, p + 1)
                        wait(lo_done, p)
                        pool.tensor_tensor(rest[:], delta_du[:], parts[0][:], ALU.subtract).then_inc(rest_done, 1)
                    if project and q == 6:
                        wait(mid_done, p + 1)
                        wait(packed_in, 16 * PARTS * JB * p)
                        pool.tensor_tensor(parts[2][:], rest[:], parts[1][:], ALU.subtract).then_inc(lo_done, 1)
                    if scan:
                        n = GROUPS * s + q
                        wait(state_done, n + 1)
                        wait(sum_done, n - 1)
                        c_all = bc[other][:, 1, :].unsqueeze(1).broadcast_to([P, JB, T])
                        pool.tensor_tensor(read[q % 2][:], state[q % 2][:], c_all, ALU.mult).then_inc(read_done, 1)
                    if ffn and q in (6, 7):
                        for m in range(len(ORDER) - RCHUNKS, len(ORDER)):
                            chunk = ORDER[m]
                            early = chunk // 2 < 4
                            if early != (q == 6):
                                continue
                            wait(h_done, CHUNKS * f + m + 1)
                            wait(pair_done, PAIRS * f + chunk // 2 + 1)
                            wait(down_mm, f)
                            pool.tensor_tensor(h[:, chunk, :], h_raw[:, chunk, :], comb_all[:, chunk, :],
                                               ALU.mult).then_inc(hc_done, 1)

            steps(pool, body)

        @block.scalar
        def _(act):
            wait = waiter(act)
            act.wait_ge(turned, 1)
            act.activation(neg_a[:], turned_a, ACT.Exp).then_inc(prep_a, 1)
            act.wait_ge(weights_ready, WEIGHT_STEPS)

            def body(k, b, project, scan, ffn):
                p, s, f = k + 1, k, k - 1
                for q in range(GROUPS):
                    if scan:
                        n = GROUPS * s + q
                        wait(delta_spread, n + 1)
                        wait(state_done, n - 1)
                        half, i = divmod(q, IN_HALF)
                        for j in range(JB):
                            g = half * (P // CH) + j * (32 // CH) + i
                            last = act.activation(decay[q % 2][:, j, 1:T], spread_ps[:, 0, j, 1:T], ACT.Exp,
                                                  scale=neg_a[:, g:g + 1])
                        last.then_inc(decay_done, 1)
                    if project and q == 0:
                        wait(xnT_mm, p + 1)
                        act.copy(xnT[:, TAPS - 1:], proj_ps[:, 0:T]).then_inc(xnT_done, 1)
                    if project and q == 1:
                        wait(conv_mm, p + 1)
                        wait(u_done, p)
                        for half in range(HALVES):
                            at = proj_ps[:, half * T:(half + 1) * T]
                            act.activation(conv_out[:, half, :], at, ACT.Identity,
                                           bias=conv_bias[:, half:half + 1])
                            last = act.activation(conv_tanh[:, half, :], at, ACT.Tanh,
                                                  bias=conv_bias_half[:, half:half + 1], scale=0.5)
                        last.then_inc(conv_act, 1)
                        wait(gate_mm, p + 1)
                        wait(gate_done, p)
                        act.activation(gate_tanh[:].rearrange("p c t -> p (c t)"), odd_ps[:], ACT.Tanh,
                                       scale=0.5).then_inc(gate_act, 1)
                    if project and q == 2:
                        wait(bc_mm, p + 1)
                        wait(read_done, GROUPS * k)
                        wait(inject_done, GROUPS * k)
                        act.copy(bc[b][:].rearrange("p c t -> p (c t)"), proj_ps[:]).then_inc(bc_done, 1)
                        wait(low_mm, p + 1)
                        act.copy(low[:], odd_ps[0:RANK, 0:T]).then_inc(low_done, 1)
                    if ffn and q == 3:
                        wait(xn2T_mm, f + 1)
                        act.copy(xn2T[:], even_ps[:, 0:T]).then_inc(xn2T_done, 1)
                    if project and q == 3:
                        wait(delta_mm, p + 1)
                        for half in range(HALVES):
                            last = act.activation(z_abs[:, half, :], proj_ps[:, half * T:(half + 1) * T], ACT.Abs,
                                                  bias=delta_b[:, half:half + 1])
                        last.then_inc(z_abs_done, 1)
                        wait(z_abs_done, p + 1)
                        wait(lost_done, 2 * p)
                        act.activation(z_exp[:], z_abs[:], ACT.Exp, scale=-1.0).then_inc(z_exp_done, 1)
                        wait(z_exp_done, p + 1)
                        wait(delta_done, p)
                        act.activation(z_log[:], z_exp[:], ACT.Ln, bias=1.0).then_inc(z_log_done, 1)
                    if ffn and q == 4:
                        wait(rank_steps, 7 * f + 4)
                        wait(comb_steps, 10 * f)
                        act.activation(expd[:], shifted[:], ACT.Exp).then_inc(expd_done, 1)
                    if ffn:
                        for m in spread(GU_SLOT, q):
                            r = rows(ORDER[m])
                            n = CHUNKS * f + m
                            bank = even_ps if m % 2 == 0 else odd_ps
                            wait(gu_mm, n + 1)
                            wait(silu_done, CHUNKS * f + max(m - 1, 0))
                            act.activation(g_tanh[m % 2][0:r, :], bank[0:r, 0:T], ACT.Tanh,
                                           scale=0.5).then_inc(tanh_done, 1)
                    if project and q == 5:
                        wait(du_done, p + 1)
                        wait(packed_in, 16 * PARTS * JB * p)
                        act.copy(parts[0][:], delta_du[:]).then_inc(hi_done, 1)
                        wait(rest_done, p + 1)
                        act.copy(parts[1][:], rest[:]).then_inc(mid_done, 1)
                    if ffn and q == 5:
                        wait(combT_mm, f + 1)
                        act.copy(combT[:], proj_ps[0:PARTS * EXPERTS, 0:P].bitcast(BF16)).then_inc(combT_done, 1)
                    if ffn:
                        for pair in spread(PAIR_SLOT, q):
                            n = PAIRS * f + pair
                            wait(pair_mm, n + 1)
                            wait(hc_done, RCHUNKS * f)
                            width = min(2, RCHUNKS - 2 * pair) * T
                            act.copy(comb_all[:, 2 * pair:2 * pair + 2, :].rearrange("p c t -> p (c t)")[:, 0:width],
                                     proj_ps[:, 0:width]).then_inc(pair_done, 1)

            steps(act, body)

        @block.vector
        def _(dve):
            wait = waiter(dve)
            for i in range(2):
                dve.memset(decay[i][:], 0.0).then_inc(prep, 1)
            dve.memset(xnT[:, 0:TAPS - 1], 0.0).then_inc(prep, 1)
            dve.wait_ge(w_loaded, 16 * len(setup_loads))
            for half in range(HALVES):
                for tap in range(TAPS):
                    dve.tensor_scalar(wconv_rows[:, half, tap, :], win_rows[:, half, :],
                                      taps[:, half, tap:tap + 1], None, ALU.mult).then_inc(prep, 1)
            dve.tensor_scalar(ffn_down[:, RCHUNKS:CHUNKS - 1, :], ffn_down[:, RCHUNKS:CHUNKS - 1, :], 0.5, None,
                              ALU.mult).then_inc(prep, 1)
            dve.tensor_scalar(ffn_down[0:LAST, CHUNKS - 1, :], ffn_down[0:LAST, CHUNKS - 1, :], 0.5, None,
                              ALU.mult).then_inc(prep, 1)
            dve.wait_ge(consts, 1)
            dve.tensor_copy(ident_bf[:], ident[:]).then_inc(prep, 1)
            dve.wait_ge(turned, 1)
            for half in range(HALVES):
                dve.tensor_copy(wconv[:, half, :, :].rearrange("d k h -> d (k h)"),
                                turned_ps[:, half, :]).then_inc(weights_ready, 1)
                dve.tensor_copy(wo[:, half, :], turned_ps[:, 2, half * P:(half + 1) * P]).then_inc(weights_ready, 1)
                dve.tensor_scalar(wout[:, half, :], turned_ps[:, 2, (2 + half) * P:(3 + half) * P], 0.5, None,
                                  ALU.mult).then_inc(weights_ready, 1)
                turned_gate = turned_ps[:, 3, half * P:half * P + RANK + 2 * STATES]
                dve.tensor_scalar(wlow[:, half, :], turned_gate[:, 0:RANK], 0.5, None,
                                  ALU.mult).then_inc(weights_ready, 1)
                for which in range(2):
                    rows_bc = turned_gate[:, RANK + which * STATES:RANK + (which + 1) * STATES]
                    dve.tensor_scalar(wbc[:, which, half, :, :], rows_bc.unsqueeze(1).broadcast_to([P, CH, STATES]),
                                      0.5, None, ALU.mult).then_inc(weights_ready, 1)
                dve.tensor_copy(wdelta[:, half, :],
                                turned_ps[0:RANK, 3, (2 + half) * P:(3 + half) * P]).then_inc(weights_ready, 1)
            dve.wait_ge(prep_a, 1)
            dve.tensor_copy(router[:], proj_ps[:, 0:EXPERTS]).then_inc(weights_ready, 1)
            dve.tensor_copy(conv_bias[:], turned_vectors[:, 0:HALVES]).then_inc(weights_ready, 1)
            dve.tensor_scalar(conv_bias_half[:], turned_vectors[:, 0:HALVES], 0.5, None,
                              ALU.mult).then_inc(weights_ready, 1)
            dve.tensor_copy(delta_b[:], turned_vectors[:, HALVES:2 * HALVES]).then_inc(weights_ready, 1)
            dve.tensor_scalar(skip_half[:], turned_vectors[:, 2 * HALVES:], 0.5, None,
                              ALU.mult).then_inc(weights_ready, 1)
            dve.tensor_scalar(neg_a[:], neg_a[:], -1.0, None, ALU.mult).then_inc(weights_ready, 1)
            dve.wait_ge(weights_ready, WEIGHT_STEPS)

            def body(k, b, project, scan, ffn):
                p, s, f = k + 1, k, k - 1
                other = 1 - b

                def layernorm_stats(source, stats, done, n):
                    for j in range(TILES):
                        dve.bn_stats(stats[:, j, :], source[:, j, :]).then_inc(done, 1)
                    wait(done, 5 * n + 2)

                def layernorm_var(stats, mean_var, var, done, n):
                    for j in range(TILES):
                        dve.bn_aggr(mean_var[:, j, :], stats[:, j, :]).then_inc(done, 1)
                    wait(done, 5 * n + 4)
                    dve.tensor_scalar(var[:], mean_var[:, :, 1], EPS, None, ALU.add).then_inc(done, 1)

                def layernorm_apply(to, source, mean_var, rstd_t, rstd_sem, done, n):
                    wait(rstd_sem, n + 1)
                    for j in range(TILES):
                        last = dve.tensor_scalar(to[:, j, :], source[:, j, :], mean_var[:, j, 0:1], rstd_t[:, j:j + 1],
                                                 ALU.subtract, ALU.mult)
                    last.then_inc(done, 1)

                def take_y(half, n, buf):
                    wait(sum_done, GROUPS * n + IN_HALF * (half + 1))
                    dve.scalar_tensor_tensor(out=y_skip[buf][:, half, :], in0=u2[buf][:, half, :],
                                             scalar=skip_half[:, half:half + 1], in1=y_ps, op0=ALU.mult,
                                             op1=ALU.add).then_inc(y_taken, 1)
                    wait(y_taken, HALVES * n + half + 1)
                    dve.memset(y_ps, 0.0).then_inc(y_clear, 1)

                for q in range(GROUPS):
                    if project and q == 0:
                        wait(x_loaded[b], 8 * (p - b) + 16)
                        layernorm_stats(x_in[b], stats1, ln1_stats, p)
                    if scan:
                        n = GROUPS * s + q
                        wait(du_spread, n + 1)
                        wait(state_done, n - 1)
                        if q == 0:
                            wait(bc_done, s + 1)
                        b_all = bc[other][:, 0, :].unsqueeze(1).broadcast_to([P, JB, T])
                        dve.tensor_tensor(inject[q % 2][:], spread_ps[:, 1, :, :], b_all,
                                          ALU.mult).then_inc(inject_done, 1)
                    if project and q == 0:
                        layernorm_var(stats1, mean_var1, var1, ln1_stats, p)
                    if ffn and q == 0:
                        take_y(HALVES - 1, f, b)
                        wait(y_taken, HALVES * f + HALVES)
                        wait(proj_mm, f)
                        dve.tensor_tensor(y_gated[:], y_skip[b][:], gate2[b][:], ALU.mult).then_inc(y_done, 1)
                    if project and q == 0:
                        wait(xnT_mm, p)
                        layernorm_apply(xn, x_in[b], mean_var1, rstd1, ln1_rstd, ln1_done, p)
                    if project and q == 1:
                        wait(conv_act, p + 1)
                        wait(y_taken, HALVES * f + HALVES)
                        dve.scalar_tensor_tensor(out=u2[b][:], in0=conv_tanh[:], scalar=1.0, in1=conv_out[:],
                                                 op0=ALU.add, op1=ALU.mult).then_inc(u_done, 1)
                        wait(gate_act, p + 1)
                        wait(y_done, f + 1)
                        dve.scalar_tensor_tensor(out=gate2[b][:].rearrange("p c t -> p (c t)"),
                                                 in0=gate_tanh[:].rearrange("p c t -> p (c t)"), scalar=1.0,
                                                 in1=odd_ps[:], op0=ALU.add, op1=ALU.mult).then_inc(gate_done, 1)
                    if ffn and q == 2:
                        wait(res_loaded[b], 8 * (f - b) + 16)
                        wait(proj_mm, f + 1)
                        wait(result_done, f)
                        dve.tensor_tensor(x1[:].rearrange("p j d -> p (j d)"), even_ps[:, 0:TILES * DIM],
                                          x_res[b][:].rearrange("p j d -> p (j d)"), ALU.add).then_inc(x1_done, 1)
                        wait(x1_done, f + 1)
                        layernorm_stats(x1, stats2, ln2_stats, f)
                    if ffn and q == 3:
                        wait(xn2T_mm, f)
                        layernorm_apply(xn2, x1, mean_var2, rstd2, ln2_rstd, ln2_done, f)
                    if project and q == 3:
                        wait(z_abs_done, p + 1)
                        wait(delta_done, p)
                        for half in range(HALVES):
                            last = dve.tensor_scalar(z_relu[:, half, :], proj_ps[:, half * T:(half + 1) * T],
                                                     delta_b[:, half:half + 1], 0.0, ALU.add, ALU.max)
                        last.then_inc(z_relu_done, 1)
                    if ffn and q == 3:
                        wait(logit_mm, f + 1)
                        dve.tensor_copy(logit[:].rearrange("p j e -> p (j e)"),
                                        odd_ps[:, 0:TILES * EXPERTS]).then_inc(rank_steps, 1)
                    if ffn and q == 4:
                        step = [7 * f + 1]

                        def then(ins):
                            step[0] = step[0] + 1
                            ins.then_inc(rank_steps, 1)

                        wait(rank_steps, step[0])
                        for j in range(TILES):
                            theirs = logit[:, j, :].unsqueeze(1).broadcast_to([P, EXPERTS, EXPERTS])
                            mine = logit[:, j, :].unsqueeze(2).broadcast_to([P, EXPERTS, EXPERTS])
                            dve.tensor_tensor(above[:, j, :, :], theirs, mine, ALU.is_gt)
                            dve.tensor_tensor(above_eq[:, j, :, :], theirs, mine, ALU.is_equal)
                        then(dve.tensor_reduce(top[:], logit[:], AX.X, ALU.max))
                        wait(rank_steps, step[0])
                        then(dve.tensor_tensor(tied[:].rearrange("p j e o -> p j (e o)"),
                                               above_eq[:].rearrange("p j e o -> p j (e o)"),
                                               before[:].rearrange("p e o -> p (e o)").unsqueeze(1)
                                               .broadcast_to([P, TILES, EXPERTS * EXPERTS]), ALU.mult))
                        then(dve.tensor_tensor(shifted[:], logit[:],
                                               top[:].unsqueeze(2).broadcast_to([P, TILES, EXPERTS]), ALU.subtract))
                        wait(rank_steps, step[0])
                        then(dve.tensor_tensor(ahead[:], tied[:], above[:], ALU.add))
                        wait(rank_steps, step[0])
                        then(dve.tensor_reduce(rank[:], ahead[:], AX.X, ALU.add))
                        wait(rank_steps, step[0])
                        then(dve.tensor_scalar(chosen[:], rank[:], 1.5, None, ALU.is_lt))
                    if project and q == 4:
                        wait(z_exp_done, p + 1)
                        wait(lost_done, 2 * p)
                        dve.tensor_scalar(kept[:], z_exp[:], 1.0, 1.0, ALU.add,
                                          ALU.subtract).then_inc(kept_done, 1)
                    if scan and q == IN_HALF:
                        take_y(0, s, other)
                    if ffn and q == 5:
                        step = [10 * f]

                        def then(ins):
                            step[0] = step[0] + 1
                            ins.then_inc(comb_steps, 1)

                        wait(expd_done, f + 1)
                        wait(rank_steps, 7 * f + 7)
                        wait(combT_mm, f)
                        then(dve.tensor_tensor(picked[:], expd[:], chosen[:], ALU.mult))
                        then(dve.tensor_reduce(total[:], expd[:], AX.X, ALU.add))
                        wait(comb_steps, step[0])
                        then(dve.tensor_reduce(picked_sum[:], picked[:], AX.X, ALU.add))
                        wait(comb_steps, step[0])
                        then(dve.scalar_tensor_tensor(out=denom[:], in0=total[:], scalar=1e-20, in1=picked_sum[:],
                                                      op0=ALU.mult, op1=ALU.add))
                        wait(comb_steps, step[0])
                        then(dve.reciprocal(inv[:], denom[:]))
                        wait(comb_steps, step[0])
                        then(dve.scalar_tensor_tensor(out=combine[:], in0=picked[:], scalar=0.5 * SCALE,
                                                      in1=inv[:].unsqueeze(2).broadcast_to([P, TILES, EXPERTS]),
                                                      op0=ALU.mult, op1=ALU.mult))
                        wait(comb_steps, step[0])
                        then(dve.tensor_copy(comb_parts[:, :, 0:EXPERTS], combine[:]))
                        wait(comb_steps, step[0])
                        then(dve.tensor_tensor(comb_r1[:], combine[:], comb_parts[:, :, 0:EXPERTS], ALU.subtract))
                        wait(comb_steps, step[0])
                        then(dve.tensor_copy(comb_parts[:, :, EXPERTS:2 * EXPERTS], comb_r1[:]))
                        wait(comb_steps, step[0])
                        then(dve.tensor_tensor(comb_parts[:, :, 2 * EXPERTS:], comb_r1[:],
                                               comb_parts[:, :, EXPERTS:2 * EXPERTS], ALU.subtract))
                    if project and q == 5:
                        wait(lost_done, 2 * p + 2)
                        wait(z_log_done, p + 1)
                        wait(rest_done, p)
                        dve.tensor_tensor(delta_du[:, :, 0:T], z_relu[:], z_log[:], ALU.add).then_inc(delta_done, 1)
                        wait(delta_done, p + 1)
                        dve.scalar_tensor_tensor(out=delta_du[:, :, T:2 * T], in0=u2[b][:], scalar=0.5,
                                                 in1=delta_du[:, :, 0:T], op0=ALU.mult,
                                                 op1=ALU.mult).then_inc(du_done, 1)
                    if ffn:
                        for m in spread(GU_SLOT, q):
                            r = rows(ORDER[m])
                            n = CHUNKS * f + m
                            bank = even_ps if m % 2 == 0 else odd_ps
                            wait(tanh_done, n + 1)
                            dve.scalar_tensor_tensor(out=g_silu[m % 2][0:r, :], in0=g_tanh[m % 2][0:r, :], scalar=1.0,
                                                     in1=bank[0:r, 0:T], op0=ALU.add,
                                                     op1=ALU.mult).then_inc(silu_done, 1)
                            wait(silu_done, n + 1)
                            if m == 0:
                                wait(down_mm, f)
                            dve.tensor_tensor(h_raw[0:r, ORDER[m], :], g_silu[m % 2][0:r, :], bank[0:r, T:2 * T],
                                              ALU.mult).then_inc(h_done, 1)
                    if scan:
                        n = GROUPS * s + q
                        wait(decay_done, n + 1)
                        wait(inject_done, n + 1)
                        wait(read_done, n - 1)
                        dve.tensor_tensor_scan(state[q % 2][:].rearrange("p j t -> p (j t)"),
                                               decay[q % 2][:].rearrange("p j t -> p (j t)"),
                                               inject[q % 2][:].rearrange("p j t -> p (j t)"), 0.0,
                                               ALU.mult, ALU.add).then_inc(state_done, 1)
                    if ffn and q == 2:
                        layernorm_var(stats2, mean_var2, var2, ln2_stats, f)
                    if ffn and q == GROUPS - 1:
                        wait(down_mm, f + 1)
                        wait(stored[b], 8 * (f - b))
                        dve.tensor_tensor(result[b][:].rearrange("p j d -> p (j d)"), down_ps,
                                          x1[:].rearrange("p j d -> p (j d)"), ALU.add).then_inc(result_done, 1)
                        wait(result_done, f + 1)
                        dve.memset(down_ps, 0.0).then_inc(down_clear, 1)

            steps(dve, body)

        @block.tensor
        def _(pe):
            wait = waiter(pe)
            pe.wait_ge(w_loaded, 16 * len(setup_loads))
            pe.wait_ge(consts, 7)
            pe.wait_ge(prep, 3 + HALVES * TAPS + 3)
            pe.wait_ge(copies_in, 16 * (PARTS - 1))
            for half in range(HALVES):
                cols = slice(half * P, (half + 1) * P)
                for tap in range(TAPS):
                    pe.transpose(turned_ps[:, half, tap * P:(tap + 1) * P], wconv_rows[:, half, tap, :], ident[:])
                pe.transpose(turned_ps[:, 2, cols], win_rows[:, HALVES + half, :], ident[:])
                pe.transpose(turned_ps[:, 2, (2 + half) * P:(3 + half) * P], wout_rows[:, cols], ident[:])
                gates = RANK + 2 * STATES
                pe.transpose(turned_ps[:, 3, half * P:half * P + gates], wgate_rows[:, cols], ident[0:gates, 0:gates])
                pe.transpose(turned_ps[0:RANK, 3, (2 + half) * P:(3 + half) * P], wdelta_rows[:, half, :], ident[:])
            pe.transpose(proj_ps[:, 0:EXPERTS], router_rows[:], ident[0:EXPERTS, 0:EXPERTS])
            pe.transpose(turned_vectors, vector_rows[:], ident[0:3 * HALVES, 0:3 * HALVES])
            pe.transpose(turned_a, a_log_rows[:], ident[0:HIDDEN // CH, 0:HIDDEN // CH])
            pe.matmul(acc_ps[:], decay[0][:, 0, 0:P], decay[0][:, 0:2, :].rearrange("p j t -> p (j t)"),
                      start=True, stop=True).then_inc(turned, 1)
            pe.wait_ge(weights_ready, WEIGHT_STEPS)

            def body(k, b, project, scan, ffn):
                p, s, f = k + 1, k, k - 1
                other = 1 - b

                def sum_states(n, q):
                    half, i = divmod(q, IN_HALF)
                    wait(read_done, GROUPS * n + q + 1)
                    if i == 0:
                        wait(y_clear, HALVES * n + half)
                    for j in range(JB):
                        last = pe.matmul(y_ps[32 * j:32 * j + 32, :], sum_sel[:, i, :], read[q % 2][:, j, :],
                                         start=False, stop=(i == IN_HALF - 1), skip_group_check=True)
                    last.then_inc(sum_done, 1)

                for q in range(GROUPS):
                    if scan:
                        n = GROUPS * s + q
                        if q == 0:
                            wait(packed_in, 16 * PARTS * JB * (s + 1))
                        half, i = divmod(q, IN_HALF)
                        for which, read_before, ready in ((0, decay_done, delta_spread),
                                                          (1, inject_done, du_spread)):
                            wait(read_before, n)
                            for j in range(0, JB, 2):
                                last = pe.matmul(spread_ps[:, which, j:j + 2, :], spread_sel[:, i, :, :],
                                                 packed[other][:, half, which, j:j + 2, :], start=True, stop=True)
                            last.then_inc(ready, 1)
                        if q > 0:
                            sum_states(s, q - 1)
                    if ffn and q == 0:
                        wait(down_clear, f)
                        sum_states(f, GROUPS - 1)
                    if project and q == 0:
                        wait(ln1_done, p + 1)
                        wait(z_abs_done, p)
                        wait(z_relu_done, p)
                        wait(pair_done, PAIRS * f)
                        for j in range(TILES):
                            last = pe.transpose(proj_ps[:, j * P:(j + 1) * P], xn[:, j, :], ident[:])
                        last.then_inc(xnT_mm, 1)
                    if project and q == 1:
                        wait(xnT_done, p + 1)
                        for half in range(HALVES):
                            for tap in range(TAPS):
                                last = pe.matmul(proj_ps[:, half * T:(half + 1) * T], wconv[:, half, tap, :],
                                                 xnT[:, tap:tap + T], start=(tap == 0), stop=(tap == TAPS - 1))
                        last.then_inc(conv_mm, 1)
                        wait(h_done, CHUNKS * f)
                        for half in range(HALVES):
                            last = pe.matmul(odd_ps[:, half * T:(half + 1) * T], wo[:, half, :],
                                             xnT[:, TAPS - 1:], start=True, stop=True)
                        last.then_inc(gate_mm, 1)
                    if ffn and q == 1:
                        wait(y_done, f + 1)
                        wait(h_done, CHUNKS * f)
                        for j in range(TILES):
                            for half in range(HALVES):
                                last = pe.matmul(even_ps[:, j * DIM:(j + 1) * DIM],
                                                 y_gated[:, half, j * P:(j + 1) * P], wout[:, half, :],
                                                 start=(half == 0), stop=(half == HALVES - 1))
                        last.then_inc(proj_mm, 1)
                    if project and q == 2:
                        wait(conv_act, p + 1)
                        wait(u_done, p + 1)
                        for which in range(2):
                            for half in range(HALVES):
                                last = pe.matmul(proj_ps[:, which * T:(which + 1) * T], wbc[:, which, half, :, :],
                                                 u2[b][:, half, :], start=(half == 0), stop=(half == HALVES - 1))
                        last.then_inc(bc_mm, 1)
                        wait(gate_done, p + 1)
                        for half in range(HALVES):
                            last = pe.matmul(odd_ps[0:RANK, 0:T], wlow[:, half, :], u2[b][:, half, :],
                                             start=(half == 0), stop=(half == HALVES - 1))
                        last.then_inc(low_mm, 1)
                    if project and q == 3:
                        wait(bc_done, p + 1)
                        wait(low_done, p + 1)
                        for half in range(HALVES):
                            last = pe.matmul(proj_ps[:, half * T:(half + 1) * T], wdelta[:, half, :], low[:],
                                             start=True, stop=True)
                        last.then_inc(delta_mm, 1)
                    if ffn and q == 3:
                        wait(ln2_done, f + 1)
                        wait(x1_done, f + 1)
                        for j in range(TILES):
                            last = pe.transpose(even_ps[:, j * P:(j + 1) * P], xn2[:, j, :], ident[:])
                        last.then_inc(xn2T_mm, 1)
                        wait(xn2T_done, f + 1)
                        if project:
                            wait(low_done, p + 1)
                        wait(h_done, CHUNKS * f)
                        for j in range(TILES):
                            last = pe.matmul(odd_ps[:, j * EXPERTS:(j + 1) * EXPERTS], xn2T[:, j * P:(j + 1) * P],
                                             router[:], start=True, stop=True)
                        last.then_inc(logit_mm, 1)
                    if ffn and q == 5:
                        wait(comb_steps, 10 * f + 10)
                        if project:
                            wait(z_abs_done, p + 1)
                            wait(z_relu_done, p + 1)
                        wait(pair_done, PAIRS * f)
                        flat = proj_ps[0:PARTS * EXPERTS, 0:P].bitcast(BF16)
                        for j in range(TILES):
                            last = pe.transpose(flat[:, j * P:(j + 1) * P], comb_parts[:, j, :], ident_bf[:])
                        last.then_inc(combT_mm, 1)
                    if ffn:
                        for m in spread(GU_SLOT, q):
                            chunk, r = ORDER[m], rows(ORDER[m])
                            n = CHUNKS * f + m
                            bank = even_ps if m % 2 == 0 else odd_ps
                            if m == 0:
                                wait(xn2T_done, f + 1)
                            elif m == 1:
                                wait(rank_steps, 7 * f + 1)
                            else:
                                wait(h_done, n - 1)
                            for side, weights in enumerate((ffn_gate, ffn_up)):
                                last = pe.matmul(bank[0:r, side * T:(side + 1) * T],
                                                 weights[:, chunk * P:chunk * P + r], xn2T[:], start=True, stop=True)
                            last.then_inc(gu_mm, 1)
                        for pair in spread(PAIR_SLOT, q):
                            n = PAIRS * f + pair
                            wait(combT_done, f + 1)
                            wait(pair_done, n)
                            for c in range(2 * pair, min(2 * pair + 2, RCHUNKS)):
                                last = pe.matmul(proj_ps[:, (c % 2) * T:(c % 2 + 1) * T],
                                                 expert_sel[:, c * P:(c + 1) * P], combT[:], start=True, stop=True)
                            last.then_inc(pair_mm, 1)
                        for m in spread(DN_SLOT, q):
                            chunk, r = ORDER[m], rows(ORDER[m])
                            if m == 0:
                                wait(down_clear, f)
                                wait(y_clear, HALVES * f + HALVES)
                                if scan:
                                    wait(y_clear, HALVES * s + 1)
                            if chunk < RCHUNKS:
                                wait(hc_done, RCHUNKS * f + chunk + 1)
                            else:
                                wait(h_done, CHUNKS * f + m + 1)
                            source = h if chunk < RCHUNKS else h_raw
                            for j in range(TILES):
                                last = pe.matmul(down_ps[:, j * DIM:(j + 1) * DIM],
                                                 source[0:r, chunk, j * P:(j + 1) * P], ffn_down[0:r, chunk, :],
                                                 start=False, stop=(m == CHUNKS - 1), skip_group_check=True)
                            if m == CHUNKS - 1:
                                last.then_inc(down_mm, 1)

            steps(pe, body)


_INS = ['L0_attn_x', 'L0_attn_W_in', 'L0_attn_conv_w', 'L0_attn_conv_b', 'L0_attn_W_gate', 'L0_attn_W_delta',
        'L0_attn_delta_bias', 'L0_attn_A_log', 'L0_attn_D', 'L0_attn_W_out', 'L0_ffn_gate_w', 'L0_ffn_w_gate',
        'L0_ffn_w_up', 'L0_ffn_w_down', 'L0_ffn_sw_gate', 'L0_ffn_sw_up', 'L0_ffn_sw_down']


def kernel(**inputs):
    import numpy as _np
    import concourse.bacc as _bacc
    from concourse import mybir as _mybir
    from concourse.bass_utils import run_bass_kernel_spmd as _run

    nc = _bacc.Bacc("TRN2", target_bir_lowering=False, num_devices=1)
    arrays, args = {}, []
    for name in _INS:
        a = _np.ascontiguousarray(inputs[name])
        arrays[f"in_{name}_dram"] = a
        args.append(nc.dram_tensor(f"in_{name}_dram", a.shape, _mybir.dt.from_np(a.dtype), kind="ExternalInput").ap())
    args.append(nc.dram_tensor("out_0_dram", (SEQS, T, DIM), _mybir.dt.float32, kind="ExternalOutput").ap())
    build(nc, *args)
    r = _run(nc, [arrays], core_ids=[0])
    return r.results[0]["out_0_dram"]
```

```python
from contextlib import ExitStack

import concourse.bass as bass
from concourse import mybir

ALU = mybir.AluOpType
ACT = mybir.ActivationFunctionType
AX = mybir.AxisListType
F32 = mybir.dt.float32
BF16 = mybir.dt.bfloat16

P = 128
SEQS, T, DIM = 32, 256, 128
HIDDEN, STATES, RANK, TAPS = 256, 16, 64, 4
HALVES = HIDDEN // P
TILES = T // P
CH = P // STATES
JB = P // 32
GROUPS = 8
IN_HALF = GROUPS // HALVES
EXPERTS, WIDTH, SHARED = 8, 176, 352
ROUTED = EXPERTS * WIDTH
FEATURES = ROUTED + SHARED
RCHUNKS = ROUTED // P
CHUNKS = -(-FEATURES // P)
LAST = FEATURES - (CHUNKS - 1) * P
ORDER = list(range(RCHUNKS, CHUNKS)) + list(range(RCHUNKS))
PARTS = 3
EPS = 1e-5
SCALE = 2.5
WEIGHT_STEPS = 7 * HALVES + 6
GU_AT = [1, 1, 2, 3, 4, 4, 4, 5, 5, 5, 6, 6, 7, 7]
HC_AT = [5, 6, 6, 7, 7, 8, 8, 8, 9, 9, 9]
DN_AT = [3, 3, 3, 6, 7, 7, 8, 8, 9, 9, 9, 10, 10, 10]
BANK = [2, 0, 2, 2, 0, 2, 1, 2, 1, 0, 1, 0, 0, 2]
BEFORE = [max((i for i in range(m) if BANK[i] == BANK[m]), default=None) for m in range(CHUNKS)]
BEFORE = [b if b is not None else max(i for i in range(CHUNKS) if BANK[i] == BANK[m]) - CHUNKS
          for m, b in enumerate(BEFORE)]


def due(slots, q):
    return [(m, at // GROUPS) for m, at in enumerate(slots) if at % GROUPS == q]


def rows(chunk):
    return P if chunk < CHUNKS - 1 else LAST


def build(nc, x, W_in, conv_w, conv_b, W_gate, W_delta, delta_bias, A_log, Dskip, W_out,
          gate_w, w_gate, w_up, w_down, sw_gate, sw_up, sw_down, out):
    with ExitStack() as ctx:
        def sb(name, shape, dt=F32):
            return ctx.enter_context(nc.sbuf_tensor(name, shape, dt))

        def sem(name):
            return ctx.enter_context(nc.semaphore(name))

        win_rows = sb("win_rows", [P, 2 * HALVES, DIM])
        taps = sb("taps", [P, HALVES, TAPS])
        wconv_rows = sb("wconv_rows", [P, HALVES, TAPS, DIM])
        wgate_rows = sb("wgate_rows", [RANK + 2 * STATES, HIDDEN])
        wdelta_rows = sb("wdelta_rows", [P, HALVES, RANK])
        wout_rows = sb("wout_rows", [DIM, HIDDEN])
        router_rows = sb("router_rows", [EXPERTS, DIM])
        conv_bias = sb("conv_bias", [P, HALVES])
        conv_bias_half = sb("conv_bias_half", [P, HALVES])
        delta_b = sb("delta_b", [P, HALVES])
        skip_half = sb("skip_half", [P, HALVES])
        vector_rows = sb("vector_rows", [3 * HALVES, P])
        a_log_rows = sb("a_log_rows", [HIDDEN // CH, P])
        neg_a = sb("neg_a", [P, HIDDEN // CH])
        wconv = sb("wconv", [DIM, HALVES, TAPS, P])
        wo = sb("wo", [DIM, HALVES, P])
        wlow = sb("wlow", [P, HALVES, RANK])
        wbc = sb("wbc", [P, 2, HALVES, CH, STATES])
        wdelta = sb("wdelta", [RANK, HALVES, P])
        wout = sb("wout", [P, HALVES, DIM])
        router = sb("router", [DIM, EXPERTS])
        ffn_gate = sb("ffn_gate", [DIM, FEATURES])
        ffn_up = sb("ffn_up", [DIM, FEATURES])
        ffn_down = sb("ffn_down", [P, CHUNKS, DIM])
        ident = sb("ident", [P, P])
        spread_sel = sb("spread_sel", [PARTS * 32, IN_HALF, CH, STATES], BF16)
        sum_sel = sb("sum_sel", [P, IN_HALF, 32])
        before = sb("before", [P, EXPERTS, EXPERTS])
        exponent = sb("exponent", [P, TILES])
        x_in = [sb(f"x_in{i}", [P, TILES, DIM]) for i in range(2)]
        stats1 = sb("stats1", [P, TILES, 6])
        mean_var1 = sb("mean_var1", [P, TILES, 2])
        var1 = sb("var1", [P, TILES])
        rstd1 = sb("rstd1", [P, TILES])
        xn = sb("xn", [P, TILES, DIM])
        xnT = sb("xnT", [DIM, TAPS - 1 + T])
        conv_out = sb("conv_out", [P, HALVES, T])
        conv_tanh = sb("conv_tanh", [P, HALVES, T])
        u2 = [sb(f"u2_{i}", [P, HALVES, T]) for i in range(2)]
        gate_tanh = sb("gate_tanh", [P, HALVES, T])
        gate2 = [sb(f"gate2_{i}", [P, HALVES, T]) for i in range(2)]
        bc = [sb(f"bc_{i}", [P, 2, T]) for i in range(2)]
        low = sb("low", [RANK, T])
        z_abs = sb("z_abs", [P, HALVES, T])
        z_exp = sb("z_exp", [P, HALVES, T])
        z_log = sb("z_log", [P, HALVES, T])
        z_relu = sb("z_relu", [P, HALVES, T])
        lost = sb("lost", [P, HALVES, T])
        kept = sb("kept", [P, HALVES, T])
        delta_du = sb("delta_du", [P, HALVES, 2 * T])
        rest = sb("rest", [P, HALVES, 2 * T])
        parts = [sb(f"part{i}", [P, HALVES, 2 * T], BF16) for i in range(PARTS)]
        packed = [sb(f"packed{i}", [PARTS * 32, HALVES, 2, JB, T], BF16) for i in range(2)]
        decay = [sb(f"decay{i}", [P, JB, T]) for i in range(2)]
        inject = [sb(f"inject{i}", [P, JB, T]) for i in range(2)]
        state = [sb(f"state{i}", [P, JB, T]) for i in range(2)]
        read = [sb(f"read{i}", [P, JB, T]) for i in range(2)]
        x_res = [sb(f"x_res{i}", [P, TILES, DIM]) for i in range(2)]
        y_skip = sb("y_skip", [P, HALVES, T])
        y_gated = sb("y_gated", [P, HALVES, T])
        x1 = [sb(f"x1_{i}", [P, TILES, DIM]) for i in range(2)]
        stats2 = sb("stats2", [P, TILES, 6])
        mean_var2 = sb("mean_var2", [P, TILES, 2])
        var2 = sb("var2", [P, TILES])
        rstd2 = sb("rstd2", [P, TILES])
        xn2 = sb("xn2", [P, TILES, DIM])
        xn2T = [sb(f"xn2T{i}", [DIM, T]) for i in range(2)]
        logit = sb("logit", [P, TILES, EXPERTS])
        above = sb("above", [P, TILES, EXPERTS, EXPERTS])
        above_eq = sb("above_eq", [P, TILES, EXPERTS, EXPERTS])
        tied = sb("tied", [P, TILES, EXPERTS, EXPERTS])
        ahead = sb("ahead", [P, TILES, EXPERTS, EXPERTS])
        rank = sb("rank", [P, TILES, EXPERTS])
        chosen = sb("chosen", [P, TILES, EXPERTS])
        top = sb("top", [P, TILES])
        shifted = sb("shifted", [P, TILES, EXPERTS])
        expd = sb("expd", [P, TILES, EXPERTS])
        total = sb("total", [P, TILES])
        picked = sb("picked", [P, TILES, EXPERTS])
        picked_sum = sb("picked_sum", [P, TILES])
        denom = sb("denom", [P, TILES])
        inv = sb("inv", [P, TILES])
        combine = sb("combine", [P, TILES, EXPERTS])
        combT = sb("combT", [EXPERTS, T])
        comb_all = sb("comb_all", [P, RCHUNKS, T])
        g_tanh = [sb(f"g_tanh{i}", [P, T]) for i in range(2)]
        g_silu = [sb(f"g_silu{i}", [P, T]) for i in range(3)]
        h_raw = sb("h_raw", [P, CHUNKS, T])
        h = sb("h", [P, RCHUNKS, T])
        result = [sb(f"result{i}", [P, TILES, DIM]) for i in range(2)]

        spread_ps = ctx.enter_context(nc.psum_tensor("spread_ps", [P, 2, JB, T], F32))
        proj_ps = ctx.enter_context(nc.psum_tensor("proj_ps", [P, 512], F32))
        even_ps = ctx.enter_context(nc.psum_tensor("even_ps", [P, 512], F32))
        odd_ps = ctx.enter_context(nc.psum_tensor("odd_ps", [P, 512], F32))
        banks = [even_ps, odd_ps, proj_ps]
        acc_ps = ctx.enter_context(nc.psum_tensor("acc_ps", [P, 512], F32))
        y_ps = acc_ps[:, 0:T]
        down_ps = acc_ps[:, T:2 * T]

        w_loaded = sem("w_loaded")
        ident_steps = sem("ident_steps")
        consts = sem("consts")
        prep = sem("prep")
        prep_a = sem("prep_a")
        turned = sem("turned")
        weights_ready = sem("weights_ready")
        x_loaded = [sem(f"x_loaded{i}") for i in range(2)]
        ln1_stats = sem("ln1_stats")
        ln1_rstd = sem("ln1_rstd")
        ln1_done = sem("ln1_done")
        xnT_mm = sem("xnT_mm")
        xnT_done = sem("xnT_done")
        conv_mm = sem("conv_mm")
        conv_act = sem("conv_act")
        u_done = sem("u_done")
        gate_mm = sem("gate_mm")
        gate_act = sem("gate_act")
        gate_done = sem("gate_done")
        bc_mm = sem("bc_mm")
        bc_done = sem("bc_done")
        low_mm = sem("low_mm")
        low_done = sem("low_done")
        delta_mm = sem("delta_mm")
        z_abs_done = sem("z_abs_done")
        z_exp_done = sem("z_exp_done")
        z_log_done = sem("z_log_done")
        z_relu_done = sem("z_relu_done")
        kept_done = sem("kept_done")
        lost_done = sem("lost_done")
        delta_done = sem("delta_done")
        du_done = sem("du_done")
        hi_done = sem("hi_done")
        rest_done = sem("rest_done")
        mid_done = sem("mid_done")
        lo_done = sem("lo_done")
        packed_in = sem("packed_in")
        delta_spread = sem("delta_spread")
        du_spread = sem("du_spread")
        decay_done = sem("decay_done")
        inject_done = sem("inject_done")
        state_done = sem("state_done")
        read_done = sem("read_done")
        sum_done = sem("sum_done")
        y_taken = sem("y_taken")
        y_clear = sem("y_clear")
        res_loaded = [sem(f"res_loaded{i}") for i in range(2)]
        y_done = sem("y_done")
        proj_mm = sem("proj_mm")
        x1_done = sem("x1_done")
        ln2_stats = sem("ln2_stats")
        ln2_rstd = sem("ln2_rstd")
        ln2_done = sem("ln2_done")
        xn2T_mm = sem("xn2T_mm")
        xn2T_done = sem("xn2T_done")
        logit_mm = sem("logit_mm")
        rank_steps = sem("rank_steps")
        expd_done = sem("expd_done")
        comb_steps = sem("comb_steps")
        combT_mm = sem("combT_mm")
        combT_done = sem("combT_done")
        comb_in = sem("comb_in")
        gu_mm = sem("gu_mm")
        tanh_done = sem("tanh_done")
        silu_done = sem("silu_done")
        h_done = sem("h_done")
        hc_done = sem("hc_done")
        down_mm = sem("down_mm")
        result_done = sem("result_done")
        down_clear = sem("down_clear")
        stored = [sem(f"stored{i}") for i in range(2)]

        x_t = x.rearrange("n (j p) d -> n p j d", p=P)
        out_t = out.rearrange("n (j p) d -> n p j d", p=P)

        setup_loads = [
            (win_rows[:], W_in.rearrange("(c p) d -> p c d", p=P)),
            (taps[:], conv_w.rearrange("(c p) o k -> p c (o k)", p=P)),
            (wgate_rows[:], W_gate),
            (wdelta_rows[:], W_delta.rearrange("(c p) r -> p c r", p=P)),
            (wout_rows[:], W_out),
            (router_rows[:], gate_w),
            (vector_rows[0:HALVES, :], conv_b.rearrange("(c p) -> c p", p=P)),
            (vector_rows[HALVES:2 * HALVES, :], delta_bias.rearrange("(c p) -> c p", p=P)),
            (vector_rows[2 * HALVES:, :], Dskip.rearrange("(c p) -> c p", p=P)),
            (a_log_rows[:], A_log.rearrange("(g c) s -> g (c s)", c=CH)),
            (ffn_gate[:, 0:ROUTED].rearrange("d (e f) -> d e f", e=EXPERTS), w_gate.rearrange("e d f -> d e f")),
            (ffn_gate[:, ROUTED:], sw_gate),
            (ffn_up[:, 0:ROUTED].rearrange("d (e f) -> d e f", e=EXPERTS), w_up.rearrange("e d f -> d e f")),
            (ffn_up[:, ROUTED:], sw_up),
            (ffn_down[:, 0:RCHUNKS, :], w_down.rearrange("e f d -> (e f) d").rearrange("(c p) d -> p c d", p=P)),
            (ffn_down[:, RCHUNKS:CHUNKS - 1, :],
             sw_down[0:SHARED - LAST, :].rearrange("(c p) d -> p c d", p=P)),
            (ffn_down[0:LAST, CHUNKS - 1, :], sw_down[SHARED - LAST:, :]),
        ]

        comb_copies = [(e, c, max(e * WIDTH, c * P), min((e + 1) * WIDTH, (c + 1) * P))
                       for e in range(EXPERTS) for c in range(RCHUNKS)
                       if max(e * WIDTH, c * P) < min((e + 1) * WIDTH, (c + 1) * P)]

        first, after = 6, SEQS - 2

        def steps(eng, body):
            def single(k):
                body(k, k % 2, lambda lag: 0 <= k + lag < SEQS)

            for k in range(-2, first):
                single(k)
            with eng.Fori(0, (after - first) // 2) as i:
                for j in range(2):
                    body(2 * i + first + j, (first + j) % 2, lambda lag: True)
            for k in range(after, SEQS + 3):
                single(k)

        def count(value):
            return max(value, 0) if isinstance(value, int) else value

        turned_ps = spread_ps[:].rearrange("p w (g h) t -> p (w g) (h t)", h=2)
        turned_vectors = proj_ps[:, 16:16 + 3 * HALVES]
        turned_a = proj_ps[:, 32:32 + HIDDEN // CH]

        block = ctx.enter_context(nc.Block())

        @block.sync
        def _(sp):
            for to, source in setup_loads:
                sp.dma_start(to, source).then_inc(w_loaded, 16)

            def body(k, odd, on):
                if on(2):
                    n, b = k + 2, odd
                    sp.wait_ge(ln1_done, count(n - 1))
                    sp.dma_start(x_in[b][:], x_t[n]).then_inc(x_loaded[b], 16)
                if on(-1):
                    n, b = k - 1, 1 - odd
                    sp.wait_ge(x1_done, count(n - 1))
                    sp.dma_start(x_res[b][:], x_t[n]).then_inc(res_loaded[b], 16)
                if on(-2):
                    n = k - 2
                    sp.wait_ge(hc_done, count(RCHUNKS * n))
                    sp.wait_ge(combT_done, n + 1)
                    for e, c, start, end in comb_copies:
                        weight = combT[e:e + 1, :].unsqueeze(1).broadcast_to([1, end - start, T])
                        sp.dma_start(comb_all[start - c * P:end - c * P, c, :], weight).then_inc(comb_in, 16)
                if on(-3):
                    n, b = k - 3, 1 - odd
                    sp.wait_ge(result_done, n + 1)
                    sp.dma_start(out_t[n], result[b][:]).then_inc(stored[b], 16)
                if on(1):
                    n, b = k + 1, 1 - odd
                    made, spread_before = n + 1, GROUPS * (n - 1)
                    sp.wait_ge(du_spread, count(spread_before))
                    for part, ready in enumerate((hi_done, mid_done, lo_done)):
                        sp.wait_ge(ready, made)
                        for j in range(JB):
                            sp.dma_start(packed[b][32 * part:32 * part + 32, :, :, j, :],
                                         parts[part][32 * j:32 * j + 32, :, :]
                                         .rearrange("p c (w t) -> p c w t", w=2)).then_inc(packed_in, 16)

            steps(sp, body)
            for b in range(2):
                sp.wait_ge(stored[b], 16 * (SEQS // 2))

        @block.gpsimd
        def _(pool):
            pool.memset(ident[:], 0.0).then_inc(ident_steps, 1)
            pool.memset(sum_sel[:], 1.0).then_inc(ident_steps, 1)
            pool.memset(before[:], 0.0).then_inc(ident_steps, 1)
            pool.memset(exponent[:], -0.5).then_inc(ident_steps, 1)
            pool.wait_ge(ident_steps, 4)
            pool.affine_select(out=ident[:], in_=ident[:], compare_op=ALU.not_equal, fill=1.0, base=0,
                               pattern=[[-1, P]], channel_multiplier=1).then_inc(consts, 1)
            pool.affine_select(out=before[:], in_=before[:], compare_op=ALU.is_ge, fill=1.0, base=0,
                               pattern=[[-1, EXPERTS], [1, EXPERTS]], channel_multiplier=0).then_inc(consts, 1)
            pool.affine_select(out=sum_sel[:], in_=sum_sel[:], compare_op=ALU.is_ge, fill=0.0, base=0,
                               pattern=[[P, IN_HALF], [-STATES, 32]], channel_multiplier=1).then_inc(ident_steps, 1)
            pool.wait_ge(ident_steps, 5)
            pool.affine_select(out=sum_sel[:], in_=sum_sel[:], compare_op=ALU.is_ge, fill=0.0, base=STATES - 1,
                               pattern=[[-P, IN_HALF], [STATES, 32]], channel_multiplier=-1).then_inc(consts, 1)
            pool.wait_ge(consts, 3)
            pool.memset(spread_sel[:], 0.0).then_inc(ident_steps, 1)
            pool.wait_ge(ident_steps, 6)
            for part in range(PARTS):
                block_rows = spread_sel[32 * part:32 * part + 32, :, :, :]
                pool.affine_select(out=block_rows, in_=block_rows, compare_op=ALU.not_equal, fill=1.0, base=0,
                                   pattern=[[-CH, IN_HALF], [-1, CH], [0, STATES]],
                                   channel_multiplier=1).then_inc(consts, 1)
                pool.wait_ge(consts, 4 + part)
            def body(k, odd, on):
                def rstd(var, rstd_t, var_sem, done, n):
                    pool.wait_ge(var_sem, 5 * n + 5)
                    pool.tensor_tensor(rstd_t[:], var[:], exponent[:], ALU.pow).then_inc(done, 1)

                def read_state(n, q, b):
                    pool.wait_ge(state_done, GROUPS * n + q + 1)
                    pool.wait_ge(sum_done, count(GROUPS * n + q - 1))
                    c_all = bc[b][:, 1, :].unsqueeze(1).broadcast_to([P, JB, T])
                    pool.tensor_tensor(read[q % 2][:], state[q % 2][:], c_all, ALU.mult).then_inc(read_done, 1)

                for q in range(GROUPS):
                    if on(-1) and q == 4:
                        rstd(var2, rstd2, ln2_stats, ln2_rstd, k - 1)
                    if on(1) and q == 4:
                        n = k + 1
                        pool.wait_ge(kept_done, n + 1)
                        pool.tensor_tensor(lost[:], z_exp[:], kept[:], ALU.subtract).then_inc(lost_done, 1)
                        pool.wait_ge(lost_done, 2 * n + 1)
                        pool.wait_ge(z_relu_done, n + 1)
                        pool.tensor_tensor(z_relu[:], z_relu[:], lost[:], ALU.add).then_inc(lost_done, 1)
                    if q == 0 and on(-1):
                        read_state(k - 1, GROUPS - 1, 1 - odd)
                    if q > 0 and on(0):
                        read_state(k, q - 1, odd)
                    if on(1) and q == 5:
                        n = k + 1
                        pool.wait_ge(hi_done, n + 1)
                        pool.wait_ge(lo_done, count(n))
                        pool.tensor_tensor(rest[:], delta_du[:], parts[0][:], ALU.subtract).then_inc(rest_done, 1)
                    if on(2) and q == 6:
                        rstd(var1, rstd1, ln1_stats, ln1_rstd, k + 2)
                    if on(1) and q == 6:
                        n = k + 1
                        pool.wait_ge(mid_done, n + 1)
                        pool.wait_ge(packed_in, count(16 * PARTS * JB * n))
                        pool.tensor_tensor(parts[2][:], rest[:], parts[1][:], ALU.subtract).then_inc(lo_done, 1)
                    for chunk, late in due(HC_AT, q):
                        if on(-2 - late):
                            n = k - 2 - late
                            m = CHUNKS - RCHUNKS + chunk
                            if chunk == 0:
                                pool.wait_ge(comb_in, count(16 * len(comb_copies) * (n + 1)))
                                pool.wait_ge(down_mm, count(n))
                            pool.wait_ge(h_done, CHUNKS * n + m + 1)
                            pool.tensor_tensor(h[:, chunk, :], h_raw[:, chunk, :], comb_all[:, chunk, :],
                                               ALU.mult).then_inc(hc_done, 1)

            steps(pool, body)

        @block.scalar
        def _(act):
            act.wait_ge(turned, 1)
            act.activation(neg_a[:], turned_a, ACT.Exp).then_inc(prep_a, 1)
            act.wait_ge(weights_ready, WEIGHT_STEPS)

            def body(k, odd, on):
                def take_bank(to, at, ready, done, n):
                    act.wait_ge(ready, n + 1)
                    act.copy(to, at).then_inc(done, 1)

                def decays(q):
                    n = GROUPS * k + q
                    act.wait_ge(delta_spread, n + 1)
                    act.wait_ge(state_done, count(n - 1))
                    half, i = divmod(q, IN_HALF)
                    for j in range(JB):
                        g = half * (P // CH) + j * (32 // CH) + i
                        last = act.activation(decay[q % 2][:, j, 1:T], spread_ps[:, 0, j, 1:T], ACT.Exp,
                                              scale=neg_a[:, g:g + 1])
                    last.then_inc(decay_done, 1)

                for q in range(GROUPS):
                    if on(1) and q == 0:
                        act.wait_ge(gate_mm, k + 1)
                        take_bank(xnT[:, TAPS - 1:], odd_ps[:, 0:T], xnT_mm, xnT_done, k + 1)
                    if on(1) and q == 1:
                        n = k + 1
                        act.wait_ge(conv_mm, n + 1)
                        act.wait_ge(u_done, count(n))
                        for half in range(HALVES):
                            at = proj_ps[:, half * T:(half + 1) * T]
                            act.activation(conv_out[:, half, :], at, ACT.Identity,
                                           bias=conv_bias[:, half:half + 1])
                            last = act.activation(conv_tanh[:, half, :], at, ACT.Tanh,
                                                  bias=conv_bias_half[:, half:half + 1], scale=0.5)
                        last.then_inc(conv_act, 1)
                    if on(1) and q == 5:
                        n = k + 1
                        act.wait_ge(du_done, n + 1)
                        act.wait_ge(packed_in, count(16 * PARTS * JB * n))
                        act.copy(parts[0][:], delta_du[:]).then_inc(hi_done, 1)
                    if on(-1) and q == 7:
                        n = k - 1
                        act.wait_ge(rank_steps, 7 * n + 4)
                        act.wait_ge(comb_steps, count(6 * n))
                        act.activation(expd[:], shifted[:], ACT.Exp).then_inc(expd_done, 1)
                    if on(0):
                        decays(q)
                    if on(-2) and q == 1:
                        n = k - 2
                        act.wait_ge(comb_in, count(16 * len(comb_copies) * n))
                        take_bank(combT[:], even_ps[0:EXPERTS, 0:T], combT_mm, combT_done, n)
                    if on(1) and q == 1:
                        n = k + 1
                        act.wait_ge(gate_mm, n + 1)
                        act.wait_ge(gate_done, count(n))
                        act.activation(gate_tanh[:].rearrange("p c t -> p (c t)"), odd_ps[:], ACT.Tanh,
                                       scale=0.5).then_inc(gate_act, 1)
                    if on(1) and q == 3:
                        n = k + 1
                        act.wait_ge(delta_mm, n + 1)
                        act.wait_ge(delta_done, count(n))
                        for half in range(HALVES):
                            at = odd_ps[:, half * T:(half + 1) * T]
                            last = act.activation(z_abs[:, half, :], at, ACT.Abs, bias=delta_b[:, half:half + 1])
                        last.then_inc(z_abs_done, 1)
                        for half in range(HALVES):
                            at = odd_ps[:, half * T:(half + 1) * T]
                            last = act.activation(z_relu[:, half, :], at, ACT.Relu, bias=delta_b[:, half:half + 1])
                        last.then_inc(z_relu_done, 1)
                        act.wait_ge(z_abs_done, n + 1)
                        act.wait_ge(lost_done, count(2 * n))
                        act.activation(z_exp[:], z_abs[:], ACT.Exp, scale=-1.0).then_inc(z_exp_done, 1)
                    if on(-1) and q == 5:
                        take_bank(xn2T[1 - odd][:], even_ps[:, 0:T], xn2T_mm, xn2T_done, k - 1)
                    for m, late in due(GU_AT, q):
                        if on(-2 - late):
                            r, n = rows(ORDER[m]), CHUNKS * (k - 2 - late) + m
                            act.wait_ge(gu_mm, n + 1)
                            act.wait_ge(silu_done, count(n - 1))
                            act.activation(g_tanh[m % 2][0:r, :], banks[BANK[m]][0:r, 0:T], ACT.Tanh,
                                           scale=0.5).then_inc(tanh_done, 1)
                    if on(1) and q == 2:
                        n = k + 1
                        act.wait_ge(read_done, count(GROUPS * (n - 1)))
                        act.wait_ge(inject_done, count(GROUPS * (n - 1)))
                        take_bank(bc[1 - odd][:].rearrange("p c t -> p (c t)"), odd_ps[:], bc_mm, bc_done, n)
                        take_bank(low[:], even_ps[0:RANK, 0:T], low_mm, low_done, n)
                    if on(1) and q == 3:
                        n = k + 1
                        act.wait_ge(z_exp_done, n + 1)
                        act.activation(z_log[:], z_exp[:], ACT.Ln, bias=1.0).then_inc(z_log_done, 1)
                    if on(1) and q == 6:
                        n = k + 1
                        act.wait_ge(rest_done, n + 1)
                        act.copy(parts[1][:], rest[:]).then_inc(mid_done, 1)

            steps(act, body)

        @block.vector
        def _(dve):
            for i in range(2):
                dve.memset(decay[i][:], 0.0).then_inc(prep, 1)
            dve.memset(xnT[:, 0:TAPS - 1], 0.0).then_inc(prep, 1)
            dve.wait_ge(w_loaded, 16 * len(setup_loads))
            for half in range(HALVES):
                for tap in range(TAPS):
                    dve.tensor_scalar(wconv_rows[:, half, tap, :], win_rows[:, half, :],
                                      taps[:, half, tap:tap + 1], None, ALU.mult).then_inc(prep, 1)
            dve.tensor_scalar(ffn_down[:, RCHUNKS:CHUNKS - 1, :], ffn_down[:, RCHUNKS:CHUNKS - 1, :], 0.5, None,
                              ALU.mult).then_inc(prep, 1)
            dve.tensor_scalar(ffn_down[0:LAST, CHUNKS - 1, :], ffn_down[0:LAST, CHUNKS - 1, :], 0.5, None,
                              ALU.mult).then_inc(prep, 1)
            dve.wait_ge(turned, 1)
            for half in range(HALVES):
                dve.tensor_copy(wconv[:, half, :, :].rearrange("d k h -> d (k h)"),
                                turned_ps[:, half, :]).then_inc(weights_ready, 1)
                dve.tensor_copy(wo[:, half, :], turned_ps[:, 2, half * P:(half + 1) * P]).then_inc(weights_ready, 1)
                dve.tensor_scalar(wout[:, half, :], turned_ps[:, 2, (2 + half) * P:(3 + half) * P], 0.5, None,
                                  ALU.mult).then_inc(weights_ready, 1)
                turned_gate = turned_ps[:, 3, half * P:half * P + RANK + 2 * STATES]
                dve.tensor_scalar(wlow[:, half, :], turned_gate[:, 0:RANK], 0.5, None,
                                  ALU.mult).then_inc(weights_ready, 1)
                for which in range(2):
                    rows_bc = turned_gate[:, RANK + which * STATES:RANK + (which + 1) * STATES]
                    dve.tensor_scalar(wbc[:, which, half, :, :], rows_bc.unsqueeze(1).broadcast_to([P, CH, STATES]),
                                      0.5, None, ALU.mult).then_inc(weights_ready, 1)
                dve.tensor_copy(wdelta[:, half, :],
                                turned_ps[0:RANK, 3, (2 + half) * P:(3 + half) * P]).then_inc(weights_ready, 1)
            dve.wait_ge(prep_a, 1)
            dve.tensor_copy(router[:], proj_ps[:, 0:EXPERTS]).then_inc(weights_ready, 1)
            dve.tensor_copy(conv_bias[:], turned_vectors[:, 0:HALVES]).then_inc(weights_ready, 1)
            dve.tensor_scalar(conv_bias_half[:], turned_vectors[:, 0:HALVES], 0.5, None,
                              ALU.mult).then_inc(weights_ready, 1)
            dve.tensor_copy(delta_b[:], turned_vectors[:, HALVES:2 * HALVES]).then_inc(weights_ready, 1)
            dve.tensor_scalar(skip_half[:], turned_vectors[:, 2 * HALVES:], 0.5, None,
                              ALU.mult).then_inc(weights_ready, 1)
            dve.tensor_scalar(neg_a[:], neg_a[:], -1.0, None, ALU.mult).then_inc(weights_ready, 1)
            dve.wait_ge(weights_ready, WEIGHT_STEPS)

            def body(k, odd, on):
                def layernorm_stats(source, stats, done, n):
                    for j in range(TILES):
                        dve.bn_stats(stats[:, j, :], source[:, j, :]).then_inc(done, 1)
                    dve.wait_ge(done, 5 * n + 2)

                def layernorm_var(stats, mean_var, var, done, n):
                    for j in range(TILES):
                        dve.bn_aggr(mean_var[:, j, :], stats[:, j, :]).then_inc(done, 1)
                    dve.wait_ge(done, 5 * n + 4)
                    dve.tensor_scalar(var[:], mean_var[:, :, 1], EPS, None, ALU.add).then_inc(done, 1)

                def layernorm_apply(to, source, mean_var, rstd_t, rstd_sem, done, n):
                    dve.wait_ge(rstd_sem, n + 1)
                    for j in range(TILES):
                        last = dve.tensor_scalar(to[:, j, :], source[:, j, :], mean_var[:, j, 0:1], rstd_t[:, j:j + 1],
                                                 ALU.subtract, ALU.mult)
                    last.then_inc(done, 1)

                def take_y(half, n, b):
                    dve.wait_ge(sum_done, count(GROUPS * n + IN_HALF * (half + 1)))
                    dve.scalar_tensor_tensor(out=y_skip[:, half, :], in0=u2[b][:, half, :],
                                             scalar=skip_half[:, half:half + 1], in1=y_ps, op0=ALU.mult,
                                             op1=ALU.add).then_inc(y_taken, 1)
                    dve.wait_ge(y_taken, HALVES * n + half + 1)
                    dve.memset(y_ps, 0.0).then_inc(y_clear, 1)

                def recurrence(n, q):
                    group = GROUPS * n + q
                    dve.wait_ge(decay_done, group + 1)
                    dve.wait_ge(inject_done, group + 1)
                    dve.wait_ge(read_done, count(group - 1))
                    dve.tensor_tensor_scan(state[q % 2][:].rearrange("p j t -> p (j t)"),
                                           decay[q % 2][:].rearrange("p j t -> p (j t)"),
                                           inject[q % 2][:].rearrange("p j t -> p (j t)"), 0.0,
                                           ALU.mult, ALU.add).then_inc(state_done, 1)

                def injects(q):
                    n = GROUPS * k + q
                    dve.wait_ge(du_spread, n + 1)
                    dve.wait_ge(state_done, count(n - 1))
                    if q == 0:
                        dve.wait_ge(bc_done, k + 1)
                    b_all = bc[odd][:, 0, :].unsqueeze(1).broadcast_to([P, JB, T])
                    dve.tensor_tensor(inject[q % 2][:], spread_ps[:, 1, :, :], b_all,
                                      ALU.mult).then_inc(inject_done, 1)

                def silu(m, late):
                    r, n = rows(ORDER[m]), CHUNKS * (k - 2 - late) + m
                    dve.wait_ge(h_done, count(n - 1 if m < 2 else n - 2))
                    dve.wait_ge(tanh_done, n + 1)
                    dve.scalar_tensor_tensor(out=g_silu[m % 3][0:r, :], in0=g_tanh[m % 2][0:r, :], scalar=1.0,
                                             in1=banks[BANK[m]][0:r, 0:T], op0=ALU.add,
                                             op1=ALU.mult).then_inc(silu_done, 1)

                def gated_up(m, late):
                    r, n = rows(ORDER[m]), CHUNKS * (k - 2 - late) + m
                    if m == CHUNKS - RCHUNKS:
                        dve.wait_ge(hc_done, count(RCHUNKS * (k - 2 - late)))
                    dve.wait_ge(silu_done, n + 1)
                    dve.tensor_tensor(h_raw[0:r, ORDER[m], :], g_silu[m % 3][0:r, :], banks[BANK[m]][0:r, T:2 * T],
                                      ALU.mult).then_inc(h_done, 1)

                def features(m_late):
                    m_late = [(m, late) for m, late in m_late if on(-2 - late)]
                    for at, (m, late) in enumerate(m_late):
                        if at == 0:
                            silu(m, late)
                        if at + 1 < len(m_late):
                            silu(*m_late[at + 1])
                        gated_up(m, late)

                def router_step(ins):
                    ins.then_inc(rank_steps, 1)

                def comb_step(ins):
                    ins.then_inc(comb_steps, 1)

                for q in range(GROUPS):
                    if on(-2) and q == 0:
                        n = k - 2
                        dve.wait_ge(expd_done, n + 1)
                        dve.wait_ge(rank_steps, 7 * n + 7)
                        comb_step(dve.tensor_tensor(picked[:], expd[:], chosen[:], ALU.mult))
                        comb_step(dve.tensor_reduce(total[:], expd[:], AX.X, ALU.add))
                    if on(2) and q == 7:
                        n = k + 2
                        dve.wait_ge(xnT_mm, count(n))
                        layernorm_apply(xn, x_in[odd], mean_var1, rstd1, ln1_rstd, ln1_done, n)
                    if on(0) and q == 6:
                        take_y(0, k, odd)
                    if q == 0 and on(-1):
                        recurrence(k - 1, GROUPS - 1)
                    if q > 0 and on(0):
                        recurrence(k, q - 1)
                    if on(1) and q == 4:
                        n = k + 1
                        dve.wait_ge(z_exp_done, n + 1)
                        dve.wait_ge(lost_done, count(2 * n))
                        dve.tensor_scalar(kept[:], z_exp[:], 1.0, 1.0, ALU.add,
                                          ALU.subtract).then_inc(kept_done, 1)
                    if on(-2) and q == 0:
                        n = k - 2
                        dve.wait_ge(comb_steps, 6 * n + 2)
                        comb_step(dve.tensor_reduce(picked_sum[:], picked[:], AX.X, ALU.add))
                    if on(-3) and q == 3:
                        n, b = k - 3, 1 - odd
                        dve.wait_ge(down_mm, n + 1)
                        if on(0):
                            dve.wait_ge(sum_done, GROUPS * k + 1)
                        dve.wait_ge(stored[b], count(8 * (n - b)))
                        dve.tensor_tensor(result[b][:].rearrange("p j d -> p (j d)"), down_ps,
                                          x1[b][:].rearrange("p j d -> p (j d)"), ALU.add).then_inc(result_done, 1)
                        dve.wait_ge(result_done, n + 1)
                        dve.memset(down_ps, 0.0).then_inc(down_clear, 1)
                    if on(0):
                        injects(q)
                    if on(-2) and q == 0:
                        n = k - 2
                        dve.wait_ge(comb_steps, 6 * n + 3)
                        comb_step(dve.scalar_tensor_tensor(out=denom[:], in0=total[:], scalar=1e-20,
                                                           in1=picked_sum[:], op0=ALU.mult, op1=ALU.add))
                        dve.wait_ge(comb_steps, 6 * n + 4)
                        comb_step(dve.reciprocal(inv[:], denom[:]))
                        dve.wait_ge(comb_steps, 6 * n + 5)
                        dve.wait_ge(combT_mm, count(n))
                        comb_step(dve.scalar_tensor_tensor(
                            out=combine[:], in0=picked[:], scalar=0.5 * SCALE,
                            in1=inv[:].unsqueeze(2).broadcast_to([P, TILES, EXPERTS]), op0=ALU.mult, op1=ALU.mult))
                    if on(-1) and q == 1:
                        n, b = k - 1, 1 - odd
                        take_y(HALVES - 1, n, b)
                        dve.wait_ge(y_taken, HALVES * n + HALVES)
                        dve.wait_ge(proj_mm, count(n))
                        dve.tensor_tensor(y_gated[:], y_skip[:], gate2[b][:], ALU.mult).then_inc(y_done, 1)
                    if on(-1) and q == 3:
                        n, b = k - 1, 1 - odd
                        dve.wait_ge(res_loaded[b], count(8 * (n - b) + 16))
                        dve.wait_ge(proj_mm, n + 1)
                        dve.tensor_tensor(x1[b][:].rearrange("p j d -> p (j d)"), even_ps[:, 0:TILES * DIM],
                                          x_res[b][:].rearrange("p j d -> p (j d)"), ALU.add).then_inc(x1_done, 1)
                        dve.wait_ge(x1_done, n + 1)
                        layernorm_stats(x1[b], stats2, ln2_stats, n)
                    if on(-1) and q == 6:
                        n = k - 1
                        dve.wait_ge(logit_mm, n + 1)
                        dve.wait_ge(expd_done, count(n))
                        router_step(dve.tensor_copy(logit[:].rearrange("p j e -> p (j e)"),
                                                    proj_ps[:, 0:TILES * EXPERTS]))
                        dve.wait_ge(rank_steps, 7 * n + 1)
                        for j in range(TILES):
                            theirs = logit[:, j, :].unsqueeze(1).broadcast_to([P, EXPERTS, EXPERTS])
                            mine = logit[:, j, :].unsqueeze(2).broadcast_to([P, EXPERTS, EXPERTS])
                            dve.tensor_tensor(above[:, j, :, :], theirs, mine, ALU.is_gt)
                            dve.tensor_tensor(above_eq[:, j, :, :], theirs, mine, ALU.is_equal)
                        router_step(dve.tensor_reduce(top[:], logit[:], AX.X, ALU.max))
                        dve.wait_ge(rank_steps, 7 * n + 2)
                        router_step(dve.tensor_tensor(tied[:].rearrange("p j e o -> p j (e o)"),
                                                      above_eq[:].rearrange("p j e o -> p j (e o)"),
                                                      before[:].rearrange("p e o -> p (e o)").unsqueeze(1)
                                                      .broadcast_to([P, TILES, EXPERTS * EXPERTS]), ALU.mult))
                        router_step(dve.tensor_tensor(shifted[:], logit[:],
                                                      top[:].unsqueeze(2).broadcast_to([P, TILES, EXPERTS]),
                                                      ALU.subtract))
                    features(due(GU_AT, q)[0:1])
                    if on(-1) and q == 6:
                        n = k - 1
                        dve.wait_ge(rank_steps, 7 * n + 4)
                        router_step(dve.tensor_tensor(ahead[:], tied[:], above[:], ALU.add))
                    if on(-1) and q == 3:
                        layernorm_var(stats2, mean_var2, var2, ln2_stats, k - 1)
                    if on(1) and q == 1:
                        n, b = k + 1, 1 - odd
                        dve.wait_ge(conv_act, n + 1)
                        dve.scalar_tensor_tensor(out=u2[b][:], in0=conv_tanh[:], scalar=1.0, in1=conv_out[:],
                                                 op0=ALU.add, op1=ALU.mult).then_inc(u_done, 1)
                        dve.wait_ge(y_done, count(n - 1))
                        dve.wait_ge(gate_act, n + 1)
                        dve.scalar_tensor_tensor(out=gate2[b][:].rearrange("p c t -> p (c t)"),
                                                 in0=gate_tanh[:].rearrange("p c t -> p (c t)"), scalar=1.0,
                                                 in1=odd_ps[:], op0=ALU.add, op1=ALU.mult).then_inc(gate_done, 1)
                    if on(2) and q == 6:
                        n = k + 2
                        dve.wait_ge(x_loaded[odd], count(8 * (n - odd) + 16))
                        layernorm_stats(x_in[odd], stats1, ln1_stats, n)
                    features(due(GU_AT, q)[1:])
                    if on(-1) and q == 6:
                        n = k - 1
                        dve.wait_ge(rank_steps, 7 * n + 5)
                        router_step(dve.tensor_reduce(rank[:], ahead[:], AX.X, ALU.add))
                    if on(2) and q == 6:
                        layernorm_var(stats1, mean_var1, var1, ln1_stats, k + 2)
                    if on(-1) and q == 6:
                        n = k - 1
                        dve.wait_ge(rank_steps, 7 * n + 6)
                        router_step(dve.tensor_scalar(chosen[:], rank[:], 1.5, None, ALU.is_lt))
                    if on(-1) and q == 4:
                        n = k - 1
                        dve.wait_ge(xn2T_mm, count(n))
                        layernorm_apply(xn2, x1[1 - odd], mean_var2, rstd2, ln2_rstd, ln2_done, n)
                    if on(1) and q == 4:
                        n = k + 1
                        dve.wait_ge(lost_done, 2 * n + 2)
                        dve.wait_ge(z_log_done, n + 1)
                        dve.wait_ge(rest_done, count(n))
                        dve.tensor_tensor(delta_du[:, :, 0:T], z_relu[:], z_log[:], ALU.add).then_inc(delta_done, 1)
                        dve.wait_ge(delta_done, n + 1)
                        dve.scalar_tensor_tensor(out=delta_du[:, :, T:2 * T], in0=u2[1 - odd][:], scalar=0.5,
                                                 in1=delta_du[:, :, 0:T], op0=ALU.mult,
                                                 op1=ALU.mult).then_inc(du_done, 1)

            steps(dve, body)

        @block.tensor
        def _(pe):
            pe.wait_ge(w_loaded, 16 * len(setup_loads))
            pe.wait_ge(consts, 3 + PARTS)
            pe.wait_ge(prep, 3 + HALVES * TAPS + 2)
            for half in range(HALVES):
                cols = slice(half * P, (half + 1) * P)
                for tap in range(TAPS):
                    pe.transpose(turned_ps[:, half, tap * P:(tap + 1) * P], wconv_rows[:, half, tap, :], ident[:])
                pe.transpose(turned_ps[:, 2, cols], win_rows[:, HALVES + half, :], ident[:])
                pe.transpose(turned_ps[:, 2, (2 + half) * P:(3 + half) * P], wout_rows[:, cols], ident[:])
                gates = RANK + 2 * STATES
                pe.transpose(turned_ps[:, 3, half * P:half * P + gates], wgate_rows[:, cols], ident[0:gates, 0:gates])
                pe.transpose(turned_ps[0:RANK, 3, (2 + half) * P:(3 + half) * P], wdelta_rows[:, half, :], ident[:])
            pe.transpose(proj_ps[:, 0:EXPERTS], router_rows[:], ident[0:EXPERTS, 0:EXPERTS])
            pe.transpose(turned_vectors, vector_rows[:], ident[0:3 * HALVES, 0:3 * HALVES])
            pe.transpose(turned_a, a_log_rows[:], ident[0:HIDDEN // CH, 0:HIDDEN // CH])
            pe.matmul(acc_ps[:], decay[0][:, 0, 0:P], decay[0][:, 0:2, :].rearrange("p j t -> p (j t)"),
                      start=True, stop=True).then_inc(turned, 1)
            pe.wait_ge(weights_ready, WEIGHT_STEPS)

            def body(k, odd, on):
                def spread_group(q):
                    n = GROUPS * k + q
                    if q == 0:
                        pe.wait_ge(packed_in, count(16 * PARTS * JB * (k + 1)))
                    half, i = divmod(q, IN_HALF)
                    for which, read_before, ready in ((0, decay_done, delta_spread), (1, inject_done, du_spread)):
                        pe.wait_ge(read_before, count(n))
                        for j in range(0, JB, 2):
                            last = pe.matmul(spread_ps[:, which, j:j + 2, :], spread_sel[:, i, :, :],
                                             packed[odd][:, half, which, j:j + 2, :], start=True, stop=True)
                        last.then_inc(ready, 1)

                def sum_states(n, q):
                    half, i = divmod(q, IN_HALF)
                    pe.wait_ge(read_done, GROUPS * n + q + 1)
                    if i == 0:
                        pe.wait_ge(y_clear, count(HALVES * n + half))
                    for j in range(JB):
                        last = pe.matmul(y_ps[32 * j:32 * j + 32, :], sum_sel[:, i, :], read[q % 2][:, j, :],
                                         start=False, stop=(i == IN_HALF - 1), skip_group_check=True)
                    last.then_inc(sum_done, 1)

                def gate_up(m, n):
                    chunk, r, bank = ORDER[m], rows(ORDER[m]), banks[BANK[m]]
                    pe.wait_ge(h_done, count(CHUNKS * n + BEFORE[m] + 1))
                    if m == 0 and on(1):
                        pe.wait_ge(conv_act, k + 2)
                    if m == 1:
                        pe.wait_ge(combT_done, n + 1)
                    if m == 4 and on(-1):
                        pe.wait_ge(x1_done, count(k))
                    if m == 6 and on(1):
                        pe.wait_ge(z_relu_done, k + 2)
                    if m == 9 and on(-1):
                        pe.wait_ge(xn2T_done, count(k))
                    if m == 13 and on(-1):
                        pe.wait_ge(rank_steps, count(7 * (k - 1) + 1))
                    for side, weights in enumerate((ffn_gate, ffn_up)):
                        last = pe.matmul(bank[0:r, side * T:(side + 1) * T], weights[:, chunk * P:chunk * P + r],
                                         xn2T[odd][:], start=True, stop=True)
                    last.then_inc(gu_mm, 1)

                def down(m, n):
                    chunk, r = ORDER[m], rows(ORDER[m])
                    if chunk < RCHUNKS:
                        pe.wait_ge(hc_done, RCHUNKS * n + chunk + 1)
                    else:
                        pe.wait_ge(h_done, CHUNKS * n + m + 1)
                    source = h if chunk < RCHUNKS else h_raw
                    for j in range(TILES):
                        last = pe.matmul(down_ps[:, j * DIM:(j + 1) * DIM], source[0:r, chunk, j * P:(j + 1) * P],
                                         ffn_down[0:r, chunk, :], start=False, stop=(m == CHUNKS - 1),
                                         skip_group_check=True)
                    if m == CHUNKS - 1:
                        last.then_inc(down_mm, 1)

                for q in range(GROUPS):
                    if on(0):
                        spread_group(q)
                    if on(1) and q == 0:
                        n = k + 1
                        pe.wait_ge(xnT_done, n + 1)
                        if on(-2):
                            pe.wait_ge(rank_steps, count(7 * (k - 2) + 1))
                        pe.wait_ge(h_done, count(CHUNKS * (k - 2)))
                        for half in range(HALVES):
                            for tap in range(TAPS):
                                last = pe.matmul(proj_ps[:, half * T:(half + 1) * T], wconv[:, half, tap, :],
                                                 xnT[:, tap:tap + T], start=(tap == 0), stop=(tap == TAPS - 1))
                        last.then_inc(conv_mm, 1)
                    if on(-2) and q == 1:
                        n = k - 2
                        pe.wait_ge(comb_steps, 6 * n + 6)
                        pe.wait_ge(h_done, count(CHUNKS * n - 1))
                        for j in range(TILES):
                            last = pe.transpose(even_ps[0:EXPERTS, j * P:(j + 1) * P], combine[:, j, :], ident[:])
                        last.then_inc(combT_mm, 1)
                    if q == 1 and on(-1):
                        sum_states(k - 1, GROUPS - 1)
                    if on(1) and q == 1:
                        n = k + 1
                        for half in range(HALVES):
                            last = pe.matmul(odd_ps[:, half * T:(half + 1) * T], wo[:, half, :],
                                             xnT[:, TAPS - 1:], start=True, stop=True)
                        last.then_inc(gate_mm, 1)
                    if on(1) and q == 3:
                        n = k + 1
                        pe.wait_ge(bc_done, n + 1)
                        pe.wait_ge(low_done, n + 1)
                        for half in range(HALVES):
                            last = pe.matmul(odd_ps[:, half * T:(half + 1) * T], wdelta[:, half, :], low[:],
                                             start=True, stop=True)
                        last.then_inc(delta_mm, 1)
                    if on(-1) and q == 3:
                        n = k - 1
                        pe.wait_ge(y_done, n + 1)
                        if on(1):
                            pe.wait_ge(low_done, k + 2)
                        if on(-2):
                            pe.wait_ge(h_done, count(CHUNKS * (k - 2) + 2))
                        for j in range(TILES):
                            for half in range(HALVES):
                                last = pe.matmul(even_ps[:, j * DIM:(j + 1) * DIM],
                                                 y_gated[:, half, j * P:(j + 1) * P], wout[:, half, :],
                                                 start=(half == 0), stop=(half == HALVES - 1))
                        last.then_inc(proj_mm, 1)
                    if on(-1) and q == 5:
                        n = k - 1
                        pe.wait_ge(ln2_done, n + 1)
                        if on(-2):
                            pe.wait_ge(h_done, count(CHUNKS * (k - 2) + 5))
                        for j in range(TILES):
                            last = pe.transpose(even_ps[:, j * P:(j + 1) * P], xn2[:, j, :], ident[:])
                        last.then_inc(xn2T_mm, 1)
                    if on(-1) and q == 6:
                        n = k - 1
                        pe.wait_ge(xn2T_done, n + 1)
                        if on(-2):
                            pe.wait_ge(h_done, count(CHUNKS * (k - 2) + 8))
                        for j in range(TILES):
                            last = pe.matmul(proj_ps[:, j * EXPERTS:(j + 1) * EXPERTS],
                                             xn2T[1 - odd][:, j * P:(j + 1) * P], router[:], start=True, stop=True)
                        last.then_inc(logit_mm, 1)
                    for m, late in due(GU_AT, q):
                        if on(-2 - late):
                            gate_up(m, k - 2 - late)
                    if on(1) and q == 2:
                        n, b = k + 1, 1 - odd
                        pe.wait_ge(u_done, n + 1)
                        pe.wait_ge(gate_done, n + 1)
                        for which in range(2):
                            for half in range(HALVES):
                                last = pe.matmul(odd_ps[:, which * T:(which + 1) * T], wbc[:, which, half, :, :],
                                                 u2[b][:, half, :], start=(half == 0), stop=(half == HALVES - 1))
                        last.then_inc(bc_mm, 1)
                        if on(-2):
                            pe.wait_ge(h_done, count(CHUNKS * (k - 2) + 2))
                        for half in range(HALVES):
                            last = pe.matmul(even_ps[0:RANK, 0:T], wlow[:, half, :], u2[b][:, half, :],
                                             start=(half == 0), stop=(half == HALVES - 1))
                        last.then_inc(low_mm, 1)
                    if on(2) and q == 7:
                        n = k + 2
                        pe.wait_ge(ln1_done, n + 1)
                        if on(1):
                            pe.wait_ge(z_relu_done, k + 2)
                        if on(-2):
                            pe.wait_ge(h_done, count(CHUNKS * (k - 2) + 11))
                        for j in range(TILES):
                            last = pe.transpose(odd_ps[:, j * P:(j + 1) * P], xn[:, j, :], ident[:])
                        last.then_inc(xnT_mm, 1)
                    if q == 1 and on(-1):
                        pe.wait_ge(y_clear, count(HALVES * k))
                    if q == 3 and on(-3):
                        pe.wait_ge(down_clear, count(k - 2))
                    if q == 6 and on(0):
                        pe.wait_ge(y_clear, HALVES * k + 1)
                    for m, late in due(DN_AT, q):
                        if on(-2 - late):
                            down(m, k - 2 - late)
                    if q == 0 and on(-1):
                        sum_states(k - 1, GROUPS - 2)
                    if q > 1 and on(0):
                        sum_states(k, q - 2)

            steps(pe, body)


_INS = ['L0_attn_x', 'L0_attn_W_in', 'L0_attn_conv_w', 'L0_attn_conv_b', 'L0_attn_W_gate', 'L0_attn_W_delta',
        'L0_attn_delta_bias', 'L0_attn_A_log', 'L0_attn_D', 'L0_attn_W_out', 'L0_ffn_gate_w', 'L0_ffn_w_gate',
        'L0_ffn_w_up', 'L0_ffn_w_down', 'L0_ffn_sw_gate', 'L0_ffn_sw_up', 'L0_ffn_sw_down']


def kernel(**inputs):
    import numpy as _np
    import concourse.bacc as _bacc
    from concourse import mybir as _mybir
    from concourse.bass_utils import run_bass_kernel_spmd as _run

    nc = _bacc.Bacc("TRN2", target_bir_lowering=False, num_devices=1)
    arrays, args = {}, []
    for name in _INS:
        a = _np.ascontiguousarray(inputs[name])
        arrays[f"in_{name}_dram"] = a
        args.append(nc.dram_tensor(f"in_{name}_dram", a.shape, _mybir.dt.from_np(a.dtype), kind="ExternalInput").ap())
    args.append(nc.dram_tensor("out_0_dram", (SEQS, T, DIM), _mybir.dt.float32, kind="ExternalOutput").ap())
    build(nc, *args)
    r = _run(nc, [arrays], core_ids=[0])
    return r.results[0]["out_0_dram"]
```

```python
from contextlib import ExitStack

import concourse.bass as bass
from concourse import mybir

ALU = mybir.AluOpType
ACT = mybir.ActivationFunctionType
AX = mybir.AxisListType
F32 = mybir.dt.float32
F32R = mybir.dt.float32r

P = 128
SEQS, T, DIM = 32, 256, 128
HIDDEN, STATES, RANK, TAPS = 256, 16, 64, 4
HALVES = HIDDEN // P
TILES = T // P
CH = P // STATES
JB = P // 32
GROUPS = 8
IN_HALF = GROUPS // HALVES
EXPERTS, WIDTH, SHARED = 8, 176, 352
ROUTED = EXPERTS * WIDTH
FEATURES = ROUTED + SHARED
RCHUNKS = ROUTED // P
CHUNKS = -(-FEATURES // P)
LAST = FEATURES - (CHUNKS - 1) * P
ORDER = list(range(RCHUNKS, CHUNKS)) + list(range(RCHUNKS))
PARTS = 2
PRODUCTS = ((0, 0), (1, 0), (0, 1))
EPS = 1e-5
SCALE = 2.5
HIGH_STEPS = 7 * HALVES + 6
WEIGHT_STEPS = HIGH_STEPS + 3 * HALVES
GU_AT = [1, 3, 3, 4, 4, 4, 5, 5, 5, 6, 6, 6, 7, 7]
HC_AT = [6, 6, 6, 7, 7, 7, 8, 8, 8, 9, 9]
DN_AT = [6, 6, 6, 7, 7, 7, 8, 9, 9, 9, 9, 9, 10, 10]
BANK = [0, 2, 0, 2, 0, 1, 2, 1, 0, 1, 0, 2, 0, 2]
BEFORE = [max((i for i in range(m) if BANK[i] == BANK[m]), default=None) for m in range(CHUNKS)]
BEFORE = [b if b is not None else max(i for i in range(CHUNKS) if BANK[i] == BANK[m]) - CHUNKS
          for m, b in enumerate(BEFORE)]


def due(slots, q):
    return [(m, at // GROUPS) for m, at in enumerate(slots) if at % GROUPS == q]


def rows(chunk):
    return P if chunk < CHUNKS - 1 else LAST


def build(nc, x, W_in, conv_w, conv_b, W_gate, W_delta, delta_bias, A_log, Dskip, W_out,
          gate_w, w_gate, w_up, w_down, sw_gate, sw_up, sw_down, out):
    with ExitStack() as ctx:
        def sb(name, shape, dt=F32):
            return ctx.enter_context(nc.sbuf_tensor(name, shape, dt))

        def sem(name):
            return ctx.enter_context(nc.semaphore(name))

        features = sb("features", [P, CHUNKS, T])
        state = sb("state", [P, 4, JB, T])
        scratch = features[:].rearrange("p c t -> p (c t)")
        wconv_rows = scratch[:, 0:1024].rearrange("p (c k d) -> p c k d", c=HALVES, k=TAPS)
        win_rows = scratch[:, 1024:1536].rearrange("p (c d) -> p c d", d=DIM)
        wgate_rows = scratch[0:RANK + 2 * STATES, 1536:1792]
        wout_rows = scratch[:, 1792:2048]
        wdelta_rows = scratch[:, 2048:2176].rearrange("p (c r) -> p c r", c=HALVES)
        router_rows = scratch[0:EXPERTS, 2176:2304]
        vector_rows = scratch[0:3 * HALVES, 2304:2432]
        a_log_rows = scratch[0:HIDDEN // CH, 2432:2560]
        sel_rows = scratch[:, 2560:3072].rearrange("p (i c s) -> p i c s", i=IN_HALF, c=CH)
        staged = state[:].rearrange("p b j t -> p (b j t)")
        gate_staged = staged[:, 0:FEATURES]
        up_staged = staged[:, FEATURES:2 * FEATURES]
        taps = sb("taps", [P, HALVES, TAPS])
        conv_bias = sb("conv_bias", [P, HALVES])
        conv_bias_half = sb("conv_bias_half", [P, HALVES])
        delta_b = sb("delta_b", [P, HALVES])
        skip_half = sb("skip_half", [P, HALVES])
        neg_a = sb("neg_a", [P, HIDDEN // CH])
        skip = sb("skip", [P, HALVES, P])
        wconv = [sb(f"wconv{i}", [DIM, HALVES, TAPS, P], F32R) for i in range(PARTS)]
        wo = [sb(f"wo{i}", [DIM, HALVES, P], F32R) for i in range(PARTS)]
        wlow = sb("wlow", [P, HALVES, RANK])
        wbc = sb("wbc", [P, 2, HALVES, CH, STATES])
        wdelta = sb("wdelta", [RANK, HALVES, P])
        wout = sb("wout", [P, HALVES, DIM])
        router = sb("router", [DIM, EXPERTS])
        ffn_gate = [sb(f"ffn_gate{i}", [DIM, FEATURES], F32R) for i in range(PARTS)]
        ffn_up = [sb(f"ffn_up{i}", [DIM, FEATURES], F32R) for i in range(PARTS)]
        ffn_down = sb("ffn_down", [P, CHUNKS, DIM])
        ident = sb("ident", [P, P])
        spread_sel = sb("spread_sel", [P, IN_HALF, CH, STATES], F32R)
        sum_sel = sb("sum_sel", [P, IN_HALF, 32])
        before = sb("before", [P, EXPERTS, EXPERTS])
        exponent = sb("exponent", [P, TILES])
        x_in = [sb(f"x_in{i}", [P, TILES, DIM]) for i in range(2)]
        stats1 = sb("stats1", [P, TILES, 6])
        mean_var1 = sb("mean_var1", [P, TILES, 2])
        var1 = sb("var1", [P, TILES])
        neg_mean1 = sb("neg_mean1", [P, TILES])
        rstd1 = sb("rstd1", [P, TILES])
        xn = sb("xn", [P, TILES, DIM])
        shift1 = sb("shift1", [P, TILES])
        xnT = sb("xnT", [DIM, T])
        xnT_parts = [sb(f"xnT_part{i}", [DIM, TAPS - 1 + T], F32R) for i in range(PARTS)]
        conv_out = sb("conv_out", [P, HALVES, T])
        conv_tanh = sb("conv_tanh", [P, HALVES, T])
        u2 = [sb(f"u2_{i}", [P, HALVES, T]) for i in range(2)]
        gate_tanh = sb("gate_tanh", [P, HALVES, T])
        gate2 = [sb(f"gate2_{i}", [P, HALVES, T]) for i in range(2)]
        bc = [sb(f"bc_{i}", [P, 2, T]) for i in range(2)]
        low = sb("low", [RANK, T])
        z_abs = sb("z_abs", [P, HALVES, T])
        z_log = z_abs
        z_exp = sb("z_exp", [P, HALVES, T])
        z_relu = sb("z_relu", [P, HALVES, T])
        kept = sb("kept", [P, HALVES, T])
        delta_du = sb("delta_du", [P, HALVES, 2 * T])
        parts = [sb(f"part{i}", [P, HALVES, 2 * T], F32R) for i in range(PARTS)]
        packed = [sb(f"packed{i}", [P, 2, JB, T], F32R) for i in range(2)]
        decay = [sb(f"decay{i}", [P, JB, T]) for i in range(2)]
        inject = [sb(f"inject{i}", [P, JB, T]) for i in range(2)]
        read = [sb(f"read{i}", [P, JB, T]) for i in range(2)]
        x_res = [sb(f"x_res{i}", [P, TILES, DIM]) for i in range(2)]
        y_gated = sb("y_gated", [P, HALVES, T])
        x1 = [sb(f"x1_{i}", [P, TILES, DIM]) for i in range(2)]
        stats2 = sb("stats2", [P, TILES, 6])
        mean_var2 = sb("mean_var2", [P, TILES, 2])
        var2 = sb("var2", [P, TILES])
        neg_mean2 = sb("neg_mean2", [P, TILES])
        rstd2 = sb("rstd2", [P, TILES])
        shift2 = sb("shift2", [P, TILES])
        xn2 = sb("xn2", [P, TILES, DIM])
        xn2T = sb("xn2T", [DIM, T])
        xn2T_parts = [[sb(f"xn2T{b}_part{i}", [DIM, T], F32R) for i in range(PARTS)] for b in range(2)]
        logit = sb("logit", [P, TILES, EXPERTS])
        above = sb("above", [P, TILES, EXPERTS, EXPERTS])
        above_eq = sb("above_eq", [P, TILES, EXPERTS, EXPERTS])
        tied = sb("tied", [P, TILES, EXPERTS, EXPERTS])
        ahead = sb("ahead", [P, TILES, EXPERTS, EXPERTS])
        rank = sb("rank", [P, TILES, EXPERTS])
        chosen = sb("chosen", [P, TILES, EXPERTS])
        top = sb("top", [P, TILES])
        shifted = sb("shifted", [P, TILES, EXPERTS])
        expd = sb("expd", [P, TILES, EXPERTS])
        total = sb("total", [P, TILES])
        picked = sb("picked", [P, TILES, EXPERTS])
        picked_sum = sb("picked_sum", [P, TILES])
        denom = sb("denom", [P, TILES])
        inv = sb("inv", [P, TILES])
        combine = sb("combine", [P, TILES, EXPERTS])
        combT = sb("combT", [EXPERTS, T])
        comb_all = sb("comb_all", [P, RCHUNKS, T])
        g_tanh = [sb(f"g_tanh{i}", [P, T]) for i in range(2)]
        g_silu = [sb(f"g_silu{i}", [P, T]) for i in range(3)]
        result = [sb(f"result{i}", [P, TILES, DIM]) for i in range(2)]

        spread_ps = ctx.enter_context(nc.psum_tensor("spread_ps", [P, 2, JB, T], F32))
        proj_ps = ctx.enter_context(nc.psum_tensor("proj_ps", [P, 512], F32))
        even_ps = ctx.enter_context(nc.psum_tensor("even_ps", [P, 512], F32))
        odd_ps = ctx.enter_context(nc.psum_tensor("odd_ps", [P, 512], F32))
        banks = [even_ps, odd_ps, proj_ps]
        acc_ps = ctx.enter_context(nc.psum_tensor("acc_ps", [P, 512], F32))
        y_ps = acc_ps[:, 0:T]
        down_ps = acc_ps[:, T:2 * T]

        w_loaded = sem("w_loaded")
        ident_steps = sem("ident_steps")
        consts = sem("consts")
        ffn_loaded = sem("ffn_loaded")
        ffn_high = sem("ffn_high")
        ffn_ready = sem("ffn_ready")
        prep = sem("prep")
        prep_a = sem("prep_a")
        turned = sem("turned")
        weights_ready = sem("weights_ready")
        x_loaded = [sem(f"x_loaded{i}") for i in range(2)]
        ln1_stats = sem("ln1_stats")
        ln1_rstd = sem("ln1_rstd")
        ln1_done = sem("ln1_done")
        xnT_mm = sem("xnT_mm")
        xnT_done = sem("xnT_done")
        xnT_low = sem("xnT_low")
        conv_mm = sem("conv_mm")
        conv_act = sem("conv_act")
        u_done = sem("u_done")
        gate_mm = sem("gate_mm")
        gate_act = sem("gate_act")
        gate_done = sem("gate_done")
        bc_mm = sem("bc_mm")
        bc_done = sem("bc_done")
        low_mm = sem("low_mm")
        low_done = sem("low_done")
        delta_mm = sem("delta_mm")
        z_abs_done = sem("z_abs_done")
        z_exp_done = sem("z_exp_done")
        z_log_done = sem("z_log_done")
        z_relu_done = sem("z_relu_done")
        kept_done = sem("kept_done")
        lost_done = sem("lost_done")
        delta_done = sem("delta_done")
        du_done = sem("du_done")
        hi_done = sem("hi_done")
        lo_done = sem("lo_done")
        packed_in = sem("packed_in")
        delta_spread = sem("delta_spread")
        du_spread = sem("du_spread")
        decay_done = sem("decay_done")
        inject_done = sem("inject_done")
        state_done = sem("state_done")
        read_done = sem("read_done")
        sum_done = sem("sum_done")
        y_taken = sem("y_taken")
        res_loaded = [sem(f"res_loaded{i}") for i in range(2)]
        proj_mm = sem("proj_mm")
        x1_done = sem("x1_done")
        ln2_stats = sem("ln2_stats")
        ln2_rstd = sem("ln2_rstd")
        ln2_done = sem("ln2_done")
        xn2T_mm = sem("xn2T_mm")
        xn2T_done = sem("xn2T_done")
        xn2T_low = sem("xn2T_low")
        logit_mm = sem("logit_mm")
        rank_steps = sem("rank_steps")
        expd_done = sem("expd_done")
        comb_steps = sem("comb_steps")
        combT_mm = sem("combT_mm")
        combT_done = sem("combT_done")
        comb_in = sem("comb_in")
        gu_mm = sem("gu_mm")
        tanh_done = sem("tanh_done")
        silu_done = sem("silu_done")
        h_done = sem("h_done")
        hc_done = sem("hc_done")
        down_mm = sem("down_mm")
        result_done = sem("result_done")
        stored = [sem(f"stored{i}") for i in range(2)]

        x_t = x.rearrange("n (j p) d -> n p j d", p=P)
        out_t = out.rearrange("n (j p) d -> n p j d", p=P)

        setup_loads = [
            (win_rows, W_in.rearrange("(c p) d -> p c d", p=P)),
            (taps[:], conv_w.rearrange("(c p) o k -> p c (o k)", p=P)),
            (wgate_rows, W_gate),
            (wdelta_rows, W_delta.rearrange("(c p) r -> p c r", p=P)),
            (wout_rows, W_out),
            (router_rows, gate_w),
            (vector_rows[0:HALVES, :], conv_b.rearrange("(c p) -> c p", p=P)),
            (vector_rows[HALVES:2 * HALVES, :], delta_bias.rearrange("(c p) -> c p", p=P)),
            (vector_rows[2 * HALVES:, :], Dskip.rearrange("(c p) -> c p", p=P)),
            (a_log_rows, A_log.rearrange("(g c) s -> g (c s)", c=CH)),
        ]
        ffn_loads = [
            (gate_staged[:, 0:ROUTED].rearrange("d (e f) -> d e f", e=EXPERTS), w_gate.rearrange("e d f -> d e f")),
            (gate_staged[:, ROUTED:], sw_gate),
            (up_staged[:, 0:ROUTED].rearrange("d (e f) -> d e f", e=EXPERTS), w_up.rearrange("e d f -> d e f")),
            (up_staged[:, ROUTED:], sw_up),
            (ffn_down[:, 0:RCHUNKS, :], w_down.rearrange("e f d -> (e f) d").rearrange("(c p) d -> p c d", p=P)),
            (ffn_down[:, RCHUNKS:CHUNKS - 1, :],
             sw_down[0:SHARED - LAST, :].rearrange("(c p) d -> p c d", p=P)),
            (ffn_down[0:LAST, CHUNKS - 1, :], sw_down[SHARED - LAST:, :]),
        ]

        comb_copies = [(e, c, max(e * WIDTH, c * P), min((e + 1) * WIDTH, (c + 1) * P))
                       for e in range(EXPERTS) for c in range(RCHUNKS)
                       if max(e * WIDTH, c * P) < min((e + 1) * WIDTH, (c + 1) * P)]

        first, after = 6, SEQS - 2

        def steps(eng, body):
            def single(k):
                body(k, k % 2, lambda lag: 0 <= k + lag < SEQS)

            for k in range(-2, first):
                single(k)
            with eng.Fori(0, (after - first) // 2) as i:
                for j in range(2):
                    body(2 * i + first + j, (first + j) % 2, lambda lag: True)
            for k in range(after, SEQS + 3):
                single(k)

        def count(value):
            return max(value, 0) if isinstance(value, int) else value

        turned_ps = spread_ps[:].rearrange("p w (g h) t -> p (w g) (h t)", h=2)
        turned_vectors = proj_ps[:, 16:16 + 3 * HALVES]
        turned_a = proj_ps[:, 32:32 + HIDDEN // CH]

        block = ctx.enter_context(nc.Block())

        @block.sync
        def _(sp):
            for to, source in setup_loads:
                sp.dma_start(to, source).then_inc(w_loaded, 16)

            def body(k, odd, on):
                if on(2):
                    n, b = k + 2, odd
                    sp.wait_ge(ln1_done, count(n - 1))
                    sp.dma_start(x_in[b][:], x_t[n]).then_inc(x_loaded[b], 16)
                if on(-1):
                    n, b = k - 1, 1 - odd
                    sp.wait_ge(x1_done, count(n - 1))
                    sp.dma_start(x_res[b][:], x_t[n]).then_inc(res_loaded[b], 16)
                if on(-2):
                    n = k - 2
                    sp.wait_ge(hc_done, count(RCHUNKS * n))
                    sp.wait_ge(combT_done, n + 1)
                    for e, c, start, end in comb_copies:
                        weight = combT[e:e + 1, :].unsqueeze(1).broadcast_to([1, end - start, T])
                        sp.dma_start(comb_all[start - c * P:end - c * P, c, :], weight).then_inc(comb_in, 16)
                if on(-3):
                    n, b = k - 3, 1 - odd
                    sp.wait_ge(result_done, n + 1)
                    sp.dma_start(out_t[n], result[b][:]).then_inc(stored[b], 16)
                if on(1):
                    n, b = k + 1, 1 - odd
                    made, spread_before = n + 1, GROUPS * (n - 1)
                    sp.wait_ge(du_spread, count(spread_before))
                    for part, ready in enumerate((hi_done, lo_done)):
                        sp.wait_ge(ready, made)
                        for half in range(HALVES):
                            first = 32 * (PARTS * half + part)
                            for j in range(JB):
                                sp.dma_start(packed[b][first:first + 32, :, j, :].bitcast(F32),
                                             parts[part][32 * j:32 * j + 32, half, :].bitcast(F32)
                                             .rearrange("p (w t) -> p w t", w=2)).then_inc(packed_in, 16)

            steps(sp, body)
            for b in range(2):
                sp.wait_ge(stored[b], 16 * (SEQS // 2))

        @block.gpsimd
        def _(pool):
            pool.memset(ident[:], 0.0).then_inc(ident_steps, 1)
            pool.memset(sum_sel[:], 1.0).then_inc(ident_steps, 1)
            pool.memset(before[:], 0.0).then_inc(ident_steps, 1)
            pool.memset(exponent[:], -0.5).then_inc(ident_steps, 1)
            pool.wait_ge(ident_steps, 4)
            pool.affine_select(out=ident[:], in_=ident[:], compare_op=ALU.not_equal, fill=1.0, base=0,
                               pattern=[[-1, P]], channel_multiplier=1).then_inc(consts, 1)
            pool.affine_select(out=before[:], in_=before[:], compare_op=ALU.is_ge, fill=1.0, base=0,
                               pattern=[[-1, EXPERTS], [1, EXPERTS]], channel_multiplier=0).then_inc(consts, 1)
            pool.affine_select(out=sum_sel[:], in_=sum_sel[:], compare_op=ALU.is_ge, fill=0.0, base=0,
                               pattern=[[P, IN_HALF], [-STATES, 32]], channel_multiplier=1).then_inc(ident_steps, 1)
            pool.wait_ge(ident_steps, 5)
            pool.affine_select(out=sum_sel[:], in_=sum_sel[:], compare_op=ALU.is_ge, fill=0.0, base=STATES - 1,
                               pattern=[[-P, IN_HALF], [STATES, 32]], channel_multiplier=-1).then_inc(consts, 1)
            pool.wait_ge(consts, 3)
            pool.memset(sel_rows, 0.0).then_inc(ident_steps, 1)
            pool.wait_ge(ident_steps, 6)
            for part in range(P // 32):
                block_rows = sel_rows[32 * part:32 * part + 32, :, :, :]
                pool.affine_select(out=block_rows, in_=block_rows, compare_op=ALU.not_equal, fill=1.0, base=0,
                                   pattern=[[-CH, IN_HALF], [-1, CH], [0, STATES]],
                                   channel_multiplier=1).then_inc(consts, 1)
                pool.wait_ge(consts, 4 + part)

            def body(k, odd, on):
                def rstd(var, neg_mean, rstd_t, shift, var_sem, done, n):
                    pool.wait_ge(var_sem, 6 * n + 6)
                    pool.tensor_tensor(rstd_t[:], var[:], exponent[:], ALU.pow).then_inc(done, 1)
                    pool.wait_ge(done, 2 * n + 1)
                    pool.tensor_tensor(shift[:], neg_mean[:], rstd_t[:], ALU.mult).then_inc(done, 1)

                def read_state(n, q, b):
                    pool.wait_ge(state_done, GROUPS * n + q + 1)
                    pool.wait_ge(sum_done, count(GROUPS * n + q - 1))
                    c_all = bc[b][:, 1, :].unsqueeze(1).broadcast_to([P, JB, T])
                    pool.tensor_tensor(read[q % 2][:], state[:, q % 4], c_all, ALU.mult).then_inc(read_done, 1)

                for q in range(GROUPS):
                    if on(1) and q == 0:
                        n = k + 1
                        pool.wait_ge(xnT_done, n + 1)
                        pool.tensor_tensor(xnT_parts[1][:, TAPS - 1:], xnT[:],
                                           xnT_parts[0][:, TAPS - 1:].bitcast(F32), ALU.subtract).then_inc(xnT_low, 1)
                    if on(-1) and q == 4:
                        rstd(var2, neg_mean2, rstd2, shift2, ln2_stats, ln2_rstd, k - 1)
                    for chunk, late in due(HC_AT, q):
                        if on(-2 - late):
                            n = k - 2 - late
                            m = CHUNKS - RCHUNKS + chunk
                            if chunk == 0:
                                pool.wait_ge(comb_in, count(16 * len(comb_copies) * (n + 1)))
                            pool.wait_ge(h_done, CHUNKS * n + m + 1)
                            pool.tensor_tensor(features[:, chunk, :], features[:, chunk, :], comb_all[:, chunk, :],
                                               ALU.mult).then_inc(hc_done, 1)
                    if q == 0 and on(-1):
                        read_state(k - 1, GROUPS - 1, 1 - odd)
                    if q > 0 and on(0):
                        read_state(k, q - 1, odd)
                    if on(1) and q == 3:
                        n = k + 1
                        pool.wait_ge(kept_done, n + 1)
                        pool.tensor_tensor(kept[:], z_exp[:], kept[:], ALU.subtract).then_inc(lost_done, 1)
                        pool.wait_ge(lost_done, 2 * n + 1)
                        pool.wait_ge(z_relu_done, n + 1)
                        pool.tensor_tensor(z_relu[:], z_relu[:], kept[:], ALU.add).then_inc(lost_done, 1)
                    if on(1) and q == 5:
                        n = k + 1
                        pool.wait_ge(hi_done, n + 1)
                        pool.wait_ge(packed_in, count(16 * PARTS * HALVES * JB * n))
                        pool.tensor_tensor(parts[1][:], delta_du[:], parts[0][:].bitcast(F32),
                                           ALU.subtract).then_inc(lo_done, 1)
                    if on(-1) and q == 5:
                        n = k - 1
                        pool.wait_ge(xn2T_done, n + 1)
                        pool.tensor_tensor(xn2T_parts[1 - odd][1][:], xn2T[:], xn2T_parts[1 - odd][0][:].bitcast(F32),
                                           ALU.subtract).then_inc(xn2T_low, 1)
                    if on(2) and q == 2:
                        rstd(var1, neg_mean1, rstd1, shift1, ln1_stats, ln1_rstd, k + 2)

            steps(pool, body)

        @block.scalar
        def _(act):
            act.wait_ge(x_loaded[0], 16)
            for to, source in ffn_loads:
                act.dma_start(to, source).then_inc(ffn_loaded, 16)
            act.wait_ge(turned, 1)
            act.activation(neg_a[:], turned_a, ACT.Exp).then_inc(prep_a, 1)
            act.wait_ge(weights_ready, WEIGHT_STEPS)

            def body(k, odd, on):
                def take_bank(to, at, ready, done, n):
                    act.wait_ge(ready, n + 1)
                    act.copy(to, at).then_inc(done, 1)

                def layernorm_apply(to, source, rstd_t, shift, rstd_sem, done, n):
                    act.wait_ge(rstd_sem, 2 * n + 2)
                    for j in range(TILES):
                        last = act.activation(to[:, j, :], source[:, j, :], ACT.Identity, scale=rstd_t[:, j:j + 1],
                                              bias=shift[:, j:j + 1])
                    last.then_inc(done, 1)

                def decays(q):
                    n = GROUPS * k + q
                    act.wait_ge(delta_spread, n + 1)
                    act.wait_ge(state_done, count(n - 1))
                    half, i = divmod(q, IN_HALF)
                    for j in range(JB):
                        g = half * (P // CH) + j * (32 // CH) + i
                        last = act.activation(decay[q % 2][:, j, 1:T], spread_ps[:, 0, j, 1:T], ACT.Exp,
                                              scale=neg_a[:, g:g + 1])
                    last.then_inc(decay_done, 1)

                for q in range(GROUPS):
                    if on(1) and q == 0:
                        act.wait_ge(gate_mm, k + 1)
                        act.wait_ge(xnT_mm, k + 2)
                        act.copy(xnT_parts[0][:, TAPS - 1:], odd_ps[:, 0:T])
                        act.copy(xnT[:], odd_ps[:, 0:T]).then_inc(xnT_done, 1)
                    if q == 1 and on(1) and not on(0):
                        act.wait_ge(ffn_loaded, 16 * len(ffn_loads))
                        act.copy(ffn_gate[0][:], gate_staged).then_inc(ffn_high, 1)
                        act.copy(ffn_up[0][:], up_staged).then_inc(ffn_high, 1)
                    if on(1) and q == 1:
                        n = k + 1
                        act.wait_ge(conv_mm, n + 1)
                        act.wait_ge(u_done, count(n))
                        for half in range(HALVES):
                            at = odd_ps[:, half * T:(half + 1) * T]
                            act.activation(conv_out[:, half, :], at, ACT.Identity,
                                           bias=conv_bias[:, half:half + 1])
                            last = act.activation(conv_tanh[:, half, :], at, ACT.Tanh,
                                                  bias=conv_bias_half[:, half:half + 1], scale=0.5)
                        last.then_inc(conv_act, 1)
                    if on(1) and q == 5:
                        n = k + 1
                        act.wait_ge(du_done, n + 1)
                        act.wait_ge(packed_in, count(16 * PARTS * HALVES * JB * n))
                        act.copy(parts[0][:], delta_du[:]).then_inc(hi_done, 1)
                    if on(0):
                        decays(q)
                    if on(1) and q == 4:
                        n = k + 1
                        act.wait_ge(z_exp_done, n + 1)
                        act.activation(z_log[:], z_exp[:], ACT.Ln, bias=1.0).then_inc(z_log_done, 1)
                    if on(2) and q == 6:
                        n = k + 2
                        act.wait_ge(xnT_mm, count(n))
                        layernorm_apply(xn, x_in[odd], rstd1, shift1, ln1_rstd, ln1_done, n)
                    if on(-1) and q == 4:
                        n = k - 1
                        act.wait_ge(xn2T_mm, count(n))
                        layernorm_apply(xn2, x1[1 - odd], rstd2, shift2, ln2_rstd, ln2_done, n)
                    if on(-2) and q == 1:
                        n = k - 2
                        act.wait_ge(comb_in, count(16 * len(comb_copies) * n))
                        take_bank(combT[:], even_ps[0:EXPERTS, 0:T], combT_mm, combT_done, n)
                    if on(1) and q == 1:
                        n = k + 1
                        act.wait_ge(gate_mm, n + 1)
                        act.wait_ge(gate_done, count(n))
                        act.activation(gate_tanh[:].rearrange("p c t -> p (c t)"), proj_ps[:], ACT.Tanh,
                                       scale=0.5).then_inc(gate_act, 1)
                    if on(1) and q == 3:
                        n = k + 1
                        act.wait_ge(delta_mm, n + 1)
                        act.wait_ge(delta_done, count(n))
                        for half in range(HALVES):
                            at = odd_ps[:, half * T:(half + 1) * T]
                            last = act.activation(z_abs[:, half, :], at, ACT.Abs, bias=delta_b[:, half:half + 1])
                        last.then_inc(z_abs_done, 1)
                        for half in range(HALVES):
                            at = odd_ps[:, half * T:(half + 1) * T]
                            last = act.activation(z_relu[:, half, :], at, ACT.Relu, bias=delta_b[:, half:half + 1])
                        last.then_inc(z_relu_done, 1)
                        act.wait_ge(z_abs_done, n + 1)
                        act.wait_ge(lost_done, count(2 * n))
                        act.activation(z_exp[:], z_abs[:], ACT.Exp, scale=-1.0).then_inc(z_exp_done, 1)
                    if on(-1) and q == 5:
                        n = k - 1
                        act.wait_ge(xn2T_mm, n + 1)
                        act.wait_ge(xn2T_low, count(n))
                        act.copy(xn2T_parts[1 - odd][0][:], even_ps[:, 0:T])
                        act.copy(xn2T[:], even_ps[:, 0:T]).then_inc(xn2T_done, 1)
                    for m, late in due(GU_AT, q):
                        if on(-2 - late):
                            r, n = rows(ORDER[m]), CHUNKS * (k - 2 - late) + m
                            act.wait_ge(gu_mm, n + 1)
                            act.wait_ge(silu_done, count(n - 1))
                            act.activation(g_tanh[m % 2][0:r, :], banks[BANK[m]][0:r, 0:T], ACT.Tanh,
                                           scale=0.5).then_inc(tanh_done, 1)
                    if on(-1) and q == 7:
                        n = k - 1
                        act.wait_ge(rank_steps, 7 * n + 4)
                        act.wait_ge(comb_steps, count(6 * n))
                        act.activation(expd[:], shifted[:], ACT.Exp).then_inc(expd_done, 1)
                    if on(1) and q == 2:
                        n = k + 1
                        act.wait_ge(read_done, count(GROUPS * (n - 1)))
                        act.wait_ge(inject_done, count(GROUPS * (n - 1)))
                        take_bank(bc[1 - odd][:].rearrange("p c t -> p (c t)"), odd_ps[:], bc_mm, bc_done, n)
                        take_bank(low[:], even_ps[0:RANK, 0:T], low_mm, low_done, n)

            steps(act, body)

        @block.vector
        def _(dve):
            for i in range(2):
                dve.memset(decay[i][:], 0.0).then_inc(prep, 1)
            for part in xnT_parts:
                dve.memset(part[:, 0:TAPS - 1].bitcast(F32), 0.0).then_inc(prep, 1)
            dve.wait_ge(consts, 3 + P // 32)
            dve.tensor_copy(spread_sel[:], sel_rows).then_inc(prep, 1)
            dve.wait_ge(w_loaded, 16 * len(setup_loads))
            for half in range(HALVES):
                for tap in range(TAPS):
                    dve.tensor_scalar(wconv_rows[:, half, tap, :], win_rows[:, half, :],
                                      taps[:, half, tap:tap + 1], None, ALU.mult).then_inc(prep, 1)
            dve.wait_ge(turned, 1)
            for half in range(HALVES):
                dve.tensor_copy(wconv[0][:, half, :, :].rearrange("d k h -> d (k h)"),
                                turned_ps[:, half, :]).then_inc(weights_ready, 1)
                dve.tensor_copy(wo[0][:, half, :], turned_ps[:, 2, half * P:(half + 1) * P]).then_inc(weights_ready, 1)
                dve.tensor_scalar(wout[:, half, :], turned_ps[:, 2, (2 + half) * P:(3 + half) * P], 0.5, None,
                                  ALU.mult).then_inc(weights_ready, 1)
                turned_gate = turned_ps[:, 3, half * P:half * P + RANK + 2 * STATES]
                dve.tensor_scalar(wlow[:, half, :], turned_gate[:, 0:RANK], 0.5, None,
                                  ALU.mult).then_inc(weights_ready, 1)
                for which in range(2):
                    rows_bc = turned_gate[:, RANK + which * STATES:RANK + (which + 1) * STATES]
                    dve.tensor_scalar(wbc[:, which, half, :, :], rows_bc.unsqueeze(1).broadcast_to([P, CH, STATES]),
                                      0.5, None, ALU.mult).then_inc(weights_ready, 1)
                dve.tensor_copy(wdelta[:, half, :],
                                turned_ps[0:RANK, 3, (2 + half) * P:(3 + half) * P]).then_inc(weights_ready, 1)
            dve.wait_ge(prep_a, 1)
            dve.tensor_copy(router[:], proj_ps[:, 0:EXPERTS]).then_inc(weights_ready, 1)
            dve.tensor_copy(conv_bias[:], turned_vectors[:, 0:HALVES]).then_inc(weights_ready, 1)
            dve.tensor_scalar(conv_bias_half[:], turned_vectors[:, 0:HALVES], 0.5, None,
                              ALU.mult).then_inc(weights_ready, 1)
            dve.tensor_copy(delta_b[:], turned_vectors[:, HALVES:2 * HALVES]).then_inc(weights_ready, 1)
            dve.tensor_scalar(skip_half[:], turned_vectors[:, 2 * HALVES:], 0.5, None,
                              ALU.mult).then_inc(weights_ready, 1)
            dve.tensor_scalar(neg_a[:], neg_a[:], -1.0, None, ALU.mult).then_inc(weights_ready, 1)
            dve.wait_ge(weights_ready, HIGH_STEPS)
            for half in range(HALVES):
                dve.tensor_scalar(skip[:, half, :], ident[:], skip_half[:, half:half + 1], None,
                                  ALU.mult).then_inc(weights_ready, 1)
            for half in range(HALVES):
                dve.tensor_tensor(wconv[1][:, half, :, :].rearrange("d k h -> d (k h)"), turned_ps[:, half, :],
                                  wconv[0][:, half, :, :].rearrange("d k h -> d (k h)").bitcast(F32),
                                  ALU.subtract).then_inc(weights_ready, 1)
                dve.tensor_tensor(wo[1][:, half, :], turned_ps[:, 2, half * P:(half + 1) * P],
                                  wo[0][:, half, :].bitcast(F32), ALU.subtract).then_inc(weights_ready, 1)
            dve.wait_ge(weights_ready, WEIGHT_STEPS)

            def body(k, odd, on):
                def layernorm_stats(source, stats, done, n):
                    for j in range(TILES):
                        dve.bn_stats(stats[:, j, :], source[:, j, :]).then_inc(done, 1)
                    dve.wait_ge(done, 6 * n + 2)

                def layernorm_var(stats, mean_var, var, neg_mean, done, n):
                    for j in range(TILES):
                        dve.bn_aggr(mean_var[:, j, :], stats[:, j, :]).then_inc(done, 1)
                    dve.wait_ge(done, 6 * n + 4)
                    dve.tensor_scalar(var[:], mean_var[:, :, 1], EPS, None, ALU.add).then_inc(done, 1)
                    dve.tensor_scalar(neg_mean[:], mean_var[:, :, 0], -1.0, None, ALU.mult).then_inc(done, 1)

                def take_y(half, n, b):
                    dve.wait_ge(sum_done, count(GROUPS * n + IN_HALF * (half + 1)))
                    dve.wait_ge(proj_mm, count(n))
                    dve.tensor_tensor(y_gated[:, half, :], y_ps, gate2[b][:, half, :], ALU.mult).then_inc(y_taken, 1)

                def recurrence(n, q):
                    group = GROUPS * n + q
                    dve.wait_ge(decay_done, group + 1)
                    dve.wait_ge(inject_done, group + 1)
                    dve.wait_ge(read_done, count(group - 3))
                    dve.tensor_tensor_scan(state[:, q % 4].rearrange("p j t -> p (j t)"),
                                           decay[q % 2][:].rearrange("p j t -> p (j t)"),
                                           inject[q % 2][:].rearrange("p j t -> p (j t)"), 0.0,
                                           ALU.mult, ALU.add).then_inc(state_done, 1)

                def injects(q):
                    n = GROUPS * k + q
                    dve.wait_ge(du_spread, n + 1)
                    dve.wait_ge(state_done, count(n - 1))
                    if q == 0:
                        dve.wait_ge(bc_done, k + 1)
                    b_all = bc[odd][:, 0, :].unsqueeze(1).broadcast_to([P, JB, T])
                    dve.tensor_tensor(inject[q % 2][:], spread_ps[:, 1, :, :], b_all,
                                      ALU.mult).then_inc(inject_done, 1)

                def silu(m, late):
                    r, n = rows(ORDER[m]), CHUNKS * (k - 2 - late) + m
                    dve.wait_ge(h_done, count(n - 1 if m < 2 else n - 2))
                    dve.wait_ge(tanh_done, n + 1)
                    dve.scalar_tensor_tensor(out=g_silu[m % 3][0:r, :], in0=g_tanh[m % 2][0:r, :], scalar=1.0,
                                             in1=banks[BANK[m]][0:r, 0:T], op0=ALU.add,
                                             op1=ALU.mult).then_inc(silu_done, 1)

                def gated_up(m, late):
                    r, n = rows(ORDER[m]), CHUNKS * (k - 2 - late) + m
                    dve.wait_ge(silu_done, n + 1)
                    dve.tensor_tensor(features[0:r, ORDER[m], :], g_silu[m % 3][0:r, :], banks[BANK[m]][0:r, T:2 * T],
                                      ALU.mult).then_inc(h_done, 1)

                def feature_chunks(m_late):
                    m_late = [(m, late) for m, late in m_late if on(-2 - late)]
                    for at, (m, late) in enumerate(m_late):
                        if at == 0:
                            silu(m, late)
                        if at + 1 < len(m_late):
                            silu(*m_late[at + 1])
                        gated_up(m, late)

                def router_step(ins):
                    ins.then_inc(rank_steps, 1)

                def comb_step(ins):
                    ins.then_inc(comb_steps, 1)

                for q in range(GROUPS):
                    if q == 2 and on(1) and not on(0):
                        dve.wait_ge(ffn_high, PARTS)
                        dve.tensor_tensor(ffn_gate[1][:], gate_staged, ffn_gate[0][:].bitcast(F32),
                                          ALU.subtract).then_inc(ffn_ready, 1)
                        dve.tensor_tensor(ffn_up[1][:], up_staged, ffn_up[0][:].bitcast(F32),
                                          ALU.subtract).then_inc(ffn_ready, 1)
                        dve.tensor_scalar(ffn_down[:, RCHUNKS:CHUNKS - 1, :], ffn_down[:, RCHUNKS:CHUNKS - 1, :], 0.5,
                                          None, ALU.mult).then_inc(ffn_ready, 1)
                        dve.tensor_scalar(ffn_down[0:LAST, CHUNKS - 1, :], ffn_down[0:LAST, CHUNKS - 1, :], 0.5, None,
                                          ALU.mult).then_inc(ffn_ready, 1)
                    if q == 0 and on(0) and not on(-1):
                        dve.wait_ge(ffn_ready, 4)
                    if on(-1) and q == 7:
                        n = k - 1
                        dve.wait_ge(rank_steps, 7 * n + 1)
                        for j in range(TILES):
                            theirs = logit[:, j, :].unsqueeze(1).broadcast_to([P, EXPERTS, EXPERTS])
                            mine = logit[:, j, :].unsqueeze(2).broadcast_to([P, EXPERTS, EXPERTS])
                            dve.tensor_tensor(above[:, j, :, :], theirs, mine, ALU.is_gt)
                            dve.tensor_tensor(above_eq[:, j, :, :], theirs, mine, ALU.is_equal)
                        router_step(dve.tensor_reduce(top[:], logit[:], AX.X, ALU.max))
                        dve.wait_ge(rank_steps, 7 * n + 2)
                        router_step(dve.tensor_tensor(tied[:].rearrange("p j e o -> p j (e o)"),
                                                      above_eq[:].rearrange("p j e o -> p j (e o)"),
                                                      before[:].rearrange("p e o -> p (e o)").unsqueeze(1)
                                                      .broadcast_to([P, TILES, EXPERTS * EXPERTS]), ALU.mult))
                        router_step(dve.tensor_tensor(shifted[:], logit[:],
                                                      top[:].unsqueeze(2).broadcast_to([P, TILES, EXPERTS]),
                                                      ALU.subtract))
                    if on(-2) and q == 0:
                        n = k - 2
                        dve.wait_ge(rank_steps, 7 * n + 4)
                        router_step(dve.tensor_tensor(ahead[:], tied[:], above[:], ALU.add))
                    if q == 0 and on(-1):
                        recurrence(k - 1, GROUPS - 1)
                    if on(-2) and q == 0:
                        n = k - 2
                        dve.wait_ge(rank_steps, 7 * n + 5)
                        router_step(dve.tensor_reduce(rank[:], ahead[:], AX.X, ALU.add))
                    if q not in (0, 5) and on(0):
                        recurrence(k, q - 1)
                    if on(0) and q == 6:
                        take_y(0, k, odd)
                    if on(2) and q == 2:
                        n = k + 2
                        dve.wait_ge(x_loaded[odd], count(8 * (n - odd) + 16))
                        layernorm_stats(x_in[odd], stats1, ln1_stats, n)
                    if on(-3) and q == 3:
                        n, b = k - 3, 1 - odd
                        dve.wait_ge(down_mm, n + 1)
                        if on(0):
                            dve.wait_ge(sum_done, GROUPS * k + 1)
                        dve.wait_ge(stored[b], count(8 * (n - b)))
                        dve.tensor_tensor(result[b][:].rearrange("p j d -> p (j d)"), down_ps,
                                          x1[b][:].rearrange("p j d -> p (j d)"), ALU.add).then_inc(result_done, 1)
                    if on(-1) and q == 6:
                        n = k - 1
                        dve.wait_ge(logit_mm, n + 1)
                        dve.wait_ge(expd_done, count(n))
                        router_step(dve.tensor_copy(logit[:].rearrange("p j e -> p (j e)"),
                                                    proj_ps[:, 0:TILES * EXPERTS]))
                    if on(0):
                        injects(q)
                    if on(-2) and q == 0:
                        n = k - 2
                        dve.wait_ge(rank_steps, 7 * n + 6)
                        router_step(dve.tensor_scalar(chosen[:], rank[:], 1.5, None, ALU.is_lt))
                        dve.wait_ge(expd_done, n + 1)
                        dve.wait_ge(rank_steps, 7 * n + 7)
                        comb_step(dve.tensor_tensor(picked[:], expd[:], chosen[:], ALU.mult))
                        comb_step(dve.tensor_reduce(total[:], expd[:], AX.X, ALU.add))
                        dve.wait_ge(comb_steps, 6 * n + 2)
                        comb_step(dve.tensor_reduce(picked_sum[:], picked[:], AX.X, ALU.add))
                        dve.wait_ge(comb_steps, 6 * n + 3)
                        comb_step(dve.scalar_tensor_tensor(out=denom[:], in0=total[:], scalar=1e-20,
                                                           in1=picked_sum[:], op0=ALU.mult, op1=ALU.add))
                        dve.wait_ge(comb_steps, 6 * n + 4)
                        comb_step(dve.reciprocal(inv[:], denom[:]))
                        dve.wait_ge(comb_steps, 6 * n + 5)
                        dve.wait_ge(combT_mm, count(n))
                        comb_step(dve.scalar_tensor_tensor(
                            out=combine[:], in0=picked[:], scalar=0.5 * SCALE,
                            in1=inv[:].unsqueeze(2).broadcast_to([P, TILES, EXPERTS]), op0=ALU.mult, op1=ALU.mult))
                    if on(1) and q == 4:
                        n = k + 1
                        dve.wait_ge(lost_done, 2 * n + 2)
                        dve.wait_ge(z_log_done, n + 1)
                        dve.wait_ge(lo_done, count(n))
                        dve.tensor_tensor(delta_du[:, :, 0:T], z_relu[:], z_log[:], ALU.add).then_inc(delta_done, 1)
                        dve.wait_ge(delta_done, n + 1)
                        dve.scalar_tensor_tensor(out=delta_du[:, :, T:2 * T], in0=u2[1 - odd][:], scalar=0.5,
                                                 in1=delta_du[:, :, 0:T], op0=ALU.mult,
                                                 op1=ALU.mult).then_inc(du_done, 1)
                    if on(2) and q == 2:
                        layernorm_var(stats1, mean_var1, var1, neg_mean1, ln1_stats, k + 2)
                    if on(-1) and q == 1:
                        take_y(HALVES - 1, k - 1, 1 - odd)
                    if on(-1) and q == 3:
                        n, b = k - 1, 1 - odd
                        dve.wait_ge(res_loaded[b], count(8 * (n - b) + 16))
                        dve.wait_ge(proj_mm, n + 1)
                        dve.wait_ge(result_done, count(n - 1))
                        dve.tensor_tensor(x1[b][:].rearrange("p j d -> p (j d)"), even_ps[:, 0:TILES * DIM],
                                          x_res[b][:].rearrange("p j d -> p (j d)"), ALU.add).then_inc(x1_done, 1)
                        dve.wait_ge(x1_done, n + 1)
                        layernorm_stats(x1[b], stats2, ln2_stats, n)
                    if on(0) and q == 4:
                        recurrence(k, q)
                    if on(-2) and q in (1, 3):
                        silu(GU_AT.index(q), 0)
                    if on(1) and q == 3:
                        n = k + 1
                        dve.wait_ge(z_exp_done, n + 1)
                        dve.wait_ge(lost_done, count(2 * n))
                        dve.tensor_scalar(kept[:], z_exp[:], 1.0, 1.0, ALU.add,
                                          ALU.subtract).then_inc(kept_done, 1)
                    if on(1) and q == 1:
                        n, b = k + 1, 1 - odd
                        dve.wait_ge(conv_act, n + 1)
                        dve.scalar_tensor_tensor(out=u2[b][:], in0=conv_tanh[:], scalar=1.0, in1=conv_out[:],
                                                 op0=ALU.add, op1=ALU.mult).then_inc(u_done, 1)
                    if on(-2) and q in (1, 3):
                        gated_up(GU_AT.index(q), 0)
                    if on(-1) and q == 3:
                        layernorm_var(stats2, mean_var2, var2, neg_mean2, ln2_stats, k - 1)
                    if on(1) and q == 1:
                        n, b = k + 1, 1 - odd
                        dve.wait_ge(y_taken, count(HALVES * (n - 1)))
                        dve.wait_ge(gate_act, n + 1)
                        dve.scalar_tensor_tensor(out=gate2[b][:].rearrange("p c t -> p (c t)"),
                                                 in0=gate_tanh[:].rearrange("p c t -> p (c t)"), scalar=1.0,
                                                 in1=proj_ps[:], op0=ALU.add, op1=ALU.mult).then_inc(gate_done, 1)
                    feature_chunks([c for c in due(GU_AT, q) if c[0] != GU_AT.index(q) or q not in (1, 3)])


            steps(dve, body)

        @block.tensor
        def _(pe):
            pe.wait_ge(w_loaded, 16 * len(setup_loads))
            pe.wait_ge(consts, 3)
            pe.wait_ge(prep, 2 + PARTS + 1 + HALVES * TAPS)
            for half in range(HALVES):
                cols = slice(half * P, (half + 1) * P)
                for tap in range(TAPS):
                    pe.transpose(turned_ps[:, half, tap * P:(tap + 1) * P], wconv_rows[:, half, tap, :], ident[:])
                pe.transpose(turned_ps[:, 2, cols], win_rows[:, HALVES + half, :], ident[:])
                pe.transpose(turned_ps[:, 2, (2 + half) * P:(3 + half) * P], wout_rows[:, cols], ident[:])
                gates = RANK + 2 * STATES
                pe.transpose(turned_ps[:, 3, half * P:half * P + gates], wgate_rows[:, cols], ident[0:gates, 0:gates])
                pe.transpose(turned_ps[0:RANK, 3, (2 + half) * P:(3 + half) * P], wdelta_rows[:, half, :], ident[:])
            pe.transpose(proj_ps[:, 0:EXPERTS], router_rows, ident[0:EXPERTS, 0:EXPERTS])
            pe.transpose(turned_vectors, vector_rows, ident[0:3 * HALVES, 0:3 * HALVES])
            pe.transpose(turned_a, a_log_rows, ident[0:HIDDEN // CH, 0:HIDDEN // CH]).then_inc(turned, 1)
            pe.wait_ge(weights_ready, WEIGHT_STEPS)

            def body(k, odd, on):
                def spread_group(q):
                    n = GROUPS * k + q
                    if q == 0:
                        pe.wait_ge(packed_in, count(16 * PARTS * HALVES * JB * (k + 1)))
                    half, i = divmod(q, IN_HALF)
                    at = slice(half * P // HALVES, (half + 1) * P // HALVES)
                    for which, read_before, ready in ((0, decay_done, delta_spread), (1, inject_done, du_spread)):
                        pe.wait_ge(read_before, count(n))
                        for j in range(0, JB, 2):
                            last = pe.matmul(spread_ps[:, which, j:j + 2, :], spread_sel[at, i, :, :],
                                             packed[odd][at, which, j:j + 2, :], start=True, stop=True)
                        last.then_inc(ready, 1)

                def sum_states(n, q, b):
                    half, i = divmod(q, IN_HALF)
                    pe.wait_ge(read_done, GROUPS * n + q + 1)
                    if i == 0:
                        pe.wait_ge(y_taken, count(HALVES * n + half))
                        pe.matmul(y_ps, skip[:, half, :], u2[b][:, half, :], start=True, stop=False,
                                  skip_group_check=True)
                    for j in range(JB):
                        last = pe.matmul(y_ps[32 * j:32 * j + 32, :], sum_sel[:, i, :], read[q % 2][:, j, :],
                                         start=False, stop=(i == IN_HALF - 1), skip_group_check=True)
                    last.then_inc(sum_done, 1)

                def gate_up(m, n):
                    chunk, r, bank = ORDER[m], rows(ORDER[m]), banks[BANK[m]]
                    pe.wait_ge(h_done, count(CHUNKS * n + BEFORE[m] + 1))
                    if m == 0:
                        pe.wait_ge(combT_done, n + 1)
                    if m == 1 and on(1):
                        pe.wait_ge(gate_done, k + 2)
                    if m == 2 and on(-1):
                        pe.wait_ge(x1_done, count(k))
                    if m == 5 and on(1):
                        pe.wait_ge(z_relu_done, k + 2)
                    if m == 8 and on(-1):
                        pe.wait_ge(xn2T_done, count(k))
                    if m == 11 and on(-1):
                        pe.wait_ge(rank_steps, count(7 * (k - 1) + 1))
                    pe.wait_ge(xn2T_low, n + 1)
                    for side, weights in enumerate((ffn_gate, ffn_up)):
                        for w, d in PRODUCTS:
                            last = pe.matmul(bank[0:r, side * T:(side + 1) * T],
                                             weights[w][:, chunk * P:chunk * P + r], xn2T_parts[odd][d][:],
                                             start=(w + d == 0), stop=(d == 1))
                    last.then_inc(gu_mm, 1)

                def down(m, n):
                    chunk, r = ORDER[m], rows(ORDER[m])
                    if chunk < RCHUNKS:
                        pe.wait_ge(hc_done, RCHUNKS * n + chunk + 1)
                    else:
                        pe.wait_ge(h_done, CHUNKS * n + m + 1)
                    fresh = m == 0 and not on(0)
                    for j in range(TILES):
                        last = pe.matmul(down_ps[:, j * DIM:(j + 1) * DIM], features[0:r, chunk, j * P:(j + 1) * P],
                                         ffn_down[0:r, chunk, :], start=fresh and j == 0, stop=(m == CHUNKS - 1),
                                         skip_group_check=True)
                    if m == CHUNKS - 1:
                        last.then_inc(down_mm, 1)

                def accumulate(q):
                    if q == 0 and on(-1):
                        sum_states(k - 1, GROUPS - 2, 1 - odd)
                    if q in (4, 5, 6, 7) and on(0):
                        sum_states(k, q - 2, odd)
                    if q == 1 and on(-1):
                        pe.wait_ge(y_taken, count(HALVES * k))
                    if q == 3 and on(-3):
                        pe.wait_ge(result_done, k - 2)
                    for m, late in due(DN_AT, q):
                        if on(-2 - late):
                            down(m, k - 2 - late)
                    if q in (2, 3) and on(0):
                        sum_states(k, q - 2, odd)

                for q in range(GROUPS):
                    if q == 0 and on(-2) and not on(-3):
                        pe.wait_ge(ffn_ready, 4)
                    if on(0):
                        spread_group(q)
                    if q == 1 and on(-1):
                        sum_states(k - 1, GROUPS - 1, 1 - odd)
                    if on(1) and q == 0:
                        n = k + 1
                        pe.wait_ge(xnT_done, n + 1)
                        for half in range(HALVES):
                            for w, d in PRODUCTS:
                                if d == 1:
                                    pe.wait_ge(xnT_low, n + 1)
                                for tap in range(TAPS):
                                    last = pe.matmul(odd_ps[:, half * T:(half + 1) * T], wconv[w][:, half, tap, :],
                                                     xnT_parts[d][:, tap:tap + T], start=(w + d + tap == 0),
                                                     stop=(d == 1 and tap == TAPS - 1))
                        last.then_inc(conv_mm, 1)
                    if on(-2) and q == 1:
                        n = k - 2
                        pe.wait_ge(comb_steps, 6 * n + 6)
                        pe.wait_ge(h_done, count(CHUNKS * n - 1))
                        for j in range(TILES):
                            last = pe.transpose(even_ps[0:EXPERTS, j * P:(j + 1) * P], combine[:, j, :], ident[:])
                        last.then_inc(combT_mm, 1)
                    if on(1) and q == 1:
                        n = k + 1
                        if on(-2):
                            pe.wait_ge(rank_steps, count(7 * (k - 2) + 1))
                        pe.wait_ge(h_done, count(CHUNKS * (k - 2)))
                        for half in range(HALVES):
                            for w, d in PRODUCTS:
                                last = pe.matmul(proj_ps[:, half * T:(half + 1) * T], wo[w][:, half, :],
                                                 xnT_parts[d][:, TAPS - 1:], start=(w + d == 0), stop=(d == 1))
                        last.then_inc(gate_mm, 1)
                    if on(1) and q == 3:
                        n = k + 1
                        pe.wait_ge(bc_done, n + 1)
                        pe.wait_ge(low_done, n + 1)
                        for half in range(HALVES):
                            last = pe.matmul(odd_ps[:, half * T:(half + 1) * T], wdelta[:, half, :], low[:],
                                             start=True, stop=True)
                        last.then_inc(delta_mm, 1)
                    if on(-1) and q == 3:
                        n = k - 1
                        pe.wait_ge(y_taken, HALVES * n + HALVES)
                        if on(1):
                            pe.wait_ge(low_done, k + 2)
                        if on(-2):
                            pe.wait_ge(h_done, count(CHUNKS * (k - 2) + 1))
                        for j in range(TILES):
                            for half in range(HALVES):
                                last = pe.matmul(even_ps[:, j * DIM:(j + 1) * DIM],
                                                 y_gated[:, half, j * P:(j + 1) * P], wout[:, half, :],
                                                 start=(half == 0), stop=(half == HALVES - 1))
                        last.then_inc(proj_mm, 1)
                    if on(-1) and q == 5:
                        n = k - 1
                        pe.wait_ge(ln2_done, n + 1)
                        if on(-2):
                            pe.wait_ge(h_done, count(CHUNKS * (k - 2) + 5))
                        for j in range(TILES):
                            last = pe.transpose(even_ps[:, j * P:(j + 1) * P], xn2[:, j, :], ident[:])
                        last.then_inc(xn2T_mm, 1)
                    if on(-1) and q == 6:
                        n = k - 1
                        pe.wait_ge(xn2T_done, n + 1)
                        if on(-2):
                            pe.wait_ge(h_done, count(CHUNKS * (k - 2) + 7))
                        for j in range(TILES):
                            last = pe.matmul(proj_ps[:, j * EXPERTS:(j + 1) * EXPERTS],
                                             xn2T[:, j * P:(j + 1) * P], router[:], start=True, stop=True)
                        last.then_inc(logit_mm, 1)
                    if on(2) and q == 7:
                        n = k + 2
                        pe.wait_ge(ln1_done, n + 1)
                        if on(1):
                            pe.wait_ge(z_relu_done, k + 2)
                        if on(-2):
                            pe.wait_ge(h_done, count(CHUNKS * (k - 2) + 10))
                        for j in range(TILES):
                            last = pe.transpose(odd_ps[:, j * P:(j + 1) * P], xn[:, j, :], ident[:])
                        last.then_inc(xnT_mm, 1)
                    for m, late in due(GU_AT, q):
                        if on(-2 - late):
                            gate_up(m, k - 2 - late)
                    if q == 2:
                        accumulate(q)
                    if on(1) and q == 2:
                        n, b = k + 1, 1 - odd
                        pe.wait_ge(u_done, n + 1)
                        for which in range(2):
                            for half in range(HALVES):
                                last = pe.matmul(odd_ps[:, which * T:(which + 1) * T], wbc[:, which, half, :, :],
                                                 u2[b][:, half, :], start=(half == 0), stop=(half == HALVES - 1))
                        last.then_inc(bc_mm, 1)
                        if on(-2):
                            pe.wait_ge(h_done, count(CHUNKS * (k - 2) + 1))
                        for half in range(HALVES):
                            last = pe.matmul(even_ps[0:RANK, 0:T], wlow[:, half, :], u2[b][:, half, :],
                                             start=(half == 0), stop=(half == HALVES - 1))
                        last.then_inc(low_mm, 1)
                    if q != 2:
                        accumulate(q)

            steps(pe, body)


_INS = ['L0_attn_x', 'L0_attn_W_in', 'L0_attn_conv_w', 'L0_attn_conv_b', 'L0_attn_W_gate', 'L0_attn_W_delta',
        'L0_attn_delta_bias', 'L0_attn_A_log', 'L0_attn_D', 'L0_attn_W_out', 'L0_ffn_gate_w', 'L0_ffn_w_gate',
        'L0_ffn_w_up', 'L0_ffn_w_down', 'L0_ffn_sw_gate', 'L0_ffn_sw_up', 'L0_ffn_sw_down']


def kernel(**inputs):
    import numpy as _np
    import concourse.bacc as _bacc
    from concourse import mybir as _mybir
    from concourse.bass_utils import run_bass_kernel_spmd as _run

    nc = _bacc.Bacc("TRN2", target_bir_lowering=False, num_devices=1)
    arrays, args = {}, []
    for name in _INS:
        a = _np.ascontiguousarray(inputs[name])
        arrays[f"in_{name}_dram"] = a
        args.append(nc.dram_tensor(f"in_{name}_dram", a.shape, _mybir.dt.from_np(a.dtype), kind="ExternalInput").ap())
    args.append(nc.dram_tensor("out_0_dram", (SEQS, T, DIM), _mybir.dt.float32, kind="ExternalOutput").ap())
    build(nc, *args)
    r = _run(nc, [arrays], core_ids=[0])
    return r.results[0]["out_0_dram"]
```
